# Optimizing a Trainium2 kernel written in Bass

```python
import numpy as np
import jax
import jax.numpy as jnp

def _softmax(x, axis=-1):
    return jax.nn.softmax(x, axis=axis)

def _gelu(x):
    return jax.nn.gelu(x, approximate=True)

def _silu(x):
    return jax.nn.silu(x)

def _sigmoid(x):
    return jax.nn.sigmoid(x)

def _layernorm(x, axis=-1, eps=1e-05):
    m = jnp.mean(x, axis=axis, keepdims=True)
    v = jnp.var(x, axis=axis, keepdims=True)
    return (x - m) / jnp.sqrt(v + eps)

def _scatter_add(tgt, idx, src, axis=0):
    return tgt.at[idx].add(src)

def _segment_sum(src, seg, n):
    return jax.ops.segment_sum(src, seg, n)
kernel_name = 'mk_early_fusion_embed_d1_tok_img1024_r4_1e73f5'

def setup_inputs(seed: int=0):
    np.random.seed(seed)
    _w = jnp.asarray

    def _rec_inputs():
        import jax
        import jax.numpy as jnp
        _rk = jax.random.key(seed)
        x = 7.22013e-05 + 1.00017 * jax.random.normal(jax.random.fold_in(_rk, 1), (8, 64, 256, 4), jnp.float32)
        x_txt = jax.random.randint(jax.random.fold_in(_rk, 51), (8, 128), 0, 31921, jnp.int32)
        return (x, x_txt)
    x, x_txt = _rec_inputs()

    def _L0_tok_setup():
        import jax, jax.numpy as jnp
        import numpy as np
        B, F, L, H, D = (8, 64, 256, 4, 64)
        MODEL = H * F
        WIN = 128

        def _local_mask():
            m = np.ones((L, L), dtype=bool)
            m = np.tril(m, WIN - 1)
            m = np.triu(m, -(WIN - 1))
            return jnp.asarray(m)

        def _flatten(y):
            n = y.shape[0]
            return y.transpose(0, 2, 3, 1).reshape(n, L, -1)
        key = jax.random.key(seed)
        ks = jax.random.split(key, 12)
        s = lambda n: 1.0 / np.sqrt(n)
        xav = np.sqrt(6.0 / (L + L))
        return {'x': jax.random.normal(ks[0], (B, F, L, H), jnp.float32), 'Wq_w': jax.random.normal(ks[1], (D, F), jnp.float32) * s(F), 'Wq_b': jnp.zeros((D,), jnp.float32), 'Wk_w': jax.random.normal(ks[2], (D, F), jnp.float32) * s(F), 'Wk_b': jnp.zeros((D,), jnp.float32), 'Wv_w': jax.random.normal(ks[3], (D, F), jnp.float32) * s(F), 'Wv_b': jnp.zeros((D,), jnp.float32), 'w_bias': jax.random.uniform(ks[4], (L, L), jnp.float32, -xav, xav), 'out_w': jax.random.normal(ks[5], (H * D, MODEL), jnp.float32) * s(H * D), 'out_b': jnp.zeros((MODEL,), jnp.float32), 'ln_g': jnp.ones((MODEL,), jnp.float32), 'ln_b': jnp.zeros((MODEL,), jnp.float32), 'local_mask': _local_mask()}
    _L0_tok_all = _L0_tok_setup()
    _L0_tok_in = {k: v for k, v in _L0_tok_all.items() if k in ('Wq_w', 'Wq_b', 'Wk_w', 'Wk_b', 'Wv_w', 'Wv_b', 'w_bias', 'out_w', 'out_b', 'ln_g', 'ln_b', 'local_mask')}
    del _L0_tok_all

    def _L0_txt_setup():
        import jax, jax.numpy as jnp
        import numpy as np
        VOCAB, D, H, M, L, NMAX = (8000, 256, 16, 1024, 4, 256)
        KD = D // H
        EPS = 1e-05

        def positional_encoding(n, d):
            pos = jnp.arange(n, dtype=jnp.float32)[:, None]
            div = jnp.exp(jnp.arange(0, d, 2, dtype=jnp.float32) * (-jnp.log(10000.0) / d))
            ang = pos * div
            enc = jnp.zeros((n, d), dtype=jnp.float32)
            enc = enc.at[:, 0::2].set(jnp.sin(ang))
            enc = enc.at[:, 1::2].set(jnp.cos(ang))
            return enc

        def _layernorm(z, g, b):
            mu = jnp.mean(z, axis=-1, keepdims=True)
            var = jnp.mean((z - mu) ** 2, axis=-1, keepdims=True)
            return (z - mu) * jax.lax.rsqrt(var + EPS) * g + b

        def _block(h, p):
            wq, wk, wv, wc, w1, bb1, w2, bb2, gg1, e1, gg2, e2 = p
            B, n, d = h.shape

            def heads(w):
                return (h @ w).reshape(B, n, H, KD).transpose(0, 2, 1, 3)
            Q, K, V = (heads(wq), heads(wk), heads(wv))
            scores = jnp.einsum('bhqk,bhlk->bhql', Q, K) / np.sqrt(KD).astype(np.float32)
            attn = jax.nn.softmax(scores, axis=-1)
            out = jnp.einsum('bhql,bhlv->bhqv', attn, V)
            out = out.transpose(0, 2, 1, 3).reshape(B, n, d) @ wc
            h = _layernorm(h + out, gg1, e1)
            ff = jax.nn.relu(h @ w1 + bb1) @ w2 + bb2
            return _layernorm(h + ff, gg2, e2)
        key = jax.random.key(seed)
        ks = jax.random.split(key, 12)
        s = 0.02
        return {'x': jax.random.randint(ks[0], (2, 256), 0, VOCAB), 'emb': jax.random.normal(ks[1], (VOCAB, D), jnp.float32) * s, 'Wq': jax.random.normal(ks[2], (L, D, D), jnp.float32) * s, 'Wk': jax.random.normal(ks[3], (L, D, D), jnp.float32) * s, 'Wv': jax.random.normal(ks[4], (L, D, D), jnp.float32) * s, 'Wc': jax.random.normal(ks[5], (L, D, D), jnp.float32) * s, 'W1': jax.random.normal(ks[6], (L, D, M), jnp.float32) * s, 'b1': jnp.zeros((L, M), jnp.float32), 'W2': jax.random.normal(ks[7], (L, M, D), jnp.float32) * s, 'b2': jnp.zeros((L, D), jnp.float32), 'g1': jnp.ones((L, D), jnp.float32), 'be1': jnp.zeros((L, D), jnp.float32), 'g2': jnp.ones((L, D), jnp.float32), 'be2': jnp.zeros((L, D), jnp.float32)}
    _L0_txt_all = _L0_txt_setup()
    _L0_txt_in = {k: v for k, v in _L0_txt_all.items() if k in ('emb', 'Wq', 'Wk', 'Wv', 'Wc', 'W1', 'b1', 'W2', 'b2', 'g1', 'be1', 'g2', 'be2')}
    del _L0_txt_all

    def _L0_attn_setup():
        import jax, jax.numpy as jnp
        import numpy as np
        D = 256

        def _layernorm(x, gamma, beta, eps=1e-05):
            mu = jnp.mean(x, axis=-1, keepdims=True)
            var = jnp.var(x, axis=-1, keepdims=True)
            return (x - mu) * jax.lax.rsqrt(var + eps) * gamma + beta
        key = jax.random.key(seed)
        ks = jax.random.split(key, 8)
        B, S = (4, 1024)
        hidden_states = jax.random.normal(ks[0], (B, S, D), dtype=jnp.float32)
        attention_mask = jnp.ones((B, S), dtype=jnp.int32)
        scale = 0.02
        Wq = jax.random.normal(ks[1], (D, D), jnp.float32) * scale
        bq = jnp.zeros((D,), jnp.float32)
        Wk = jax.random.normal(ks[2], (D, D), jnp.float32) * scale
        bk = jnp.zeros((D,), jnp.float32)
        Wv = jax.random.normal(ks[3], (D, D), jnp.float32) * scale
        bv = jnp.zeros((D,), jnp.float32)
        Wqa = jnp.zeros((D, D), jnp.float32)
        bqa = jnp.ones((D,), jnp.float32)
        Wka = jnp.zeros((D, D), jnp.float32)
        bka = jnp.ones((D,), jnp.float32)
        gamma = jnp.ones((D,), jnp.float32)
        beta = jnp.zeros((D,), jnp.float32)
        return {'hidden_states': hidden_states, 'attention_mask': attention_mask, 'Wq': Wq, 'bq': bq, 'Wqa': Wqa, 'bqa': bqa, 'Wk': Wk, 'bk': bk, 'Wka': Wka, 'bka': bka, 'Wv': Wv, 'bv': bv, 'gamma': gamma, 'beta': beta}
    _L0_attn_all = _L0_attn_setup()
    _L0_attn_in = {k: v for k, v in _L0_attn_all.items() if k in ('attention_mask', 'Wq', 'bq', 'Wqa', 'bqa', 'Wk', 'bk', 'Wka', 'bka', 'Wv', 'bv', 'gamma', 'beta')}
    del _L0_attn_all

    def _L0_ffn_setup():
        import jax, jax.numpy as jnp
        import numpy as np
        N_EXP = 8
        TOP_K = 2
        CAP_FACTOR = 1.25
        NEG_INF = -1000000000.0

        def _moe_forward(x, w_g, c_fc, c_proj):
            B, T, D = x.shape
            N = B * T
            xf = x.reshape(N, D)
            logits = xf @ w_g
            topv, topi = jax.lax.top_k(logits, TOP_K)
            full = jnp.full_like(logits, NEG_INF)
            full = full.at[jnp.arange(N)[:, None], topi].set(topv)
            probs = jax.nn.softmax(full, axis=-1)
            capacity = int(TOP_K * CAP_FACTOR * N / N_EXP)
            capacity += capacity % 2
            mask = jax.nn.one_hot(jnp.swapaxes(topi, 0, 1), N_EXP, dtype=jnp.int32)
            rank = jnp.cumsum(mask.reshape(TOP_K * N, N_EXP), axis=0).reshape(TOP_K, N, N_EXP) - 1
            mask = mask * (rank < capacity)
            rank_sel = jnp.sum(mask * rank, axis=-1)
            wts = jnp.sum(mask * probs[None], axis=-1)
            cb = jnp.zeros((N, N_EXP, capacity), x.dtype)
            tok = jnp.arange(N)
            for k in range(TOP_K):
                cb = cb.at[tok, topi[:, k], rank_sel[k]].add(wts[k])
            sec_mask = (cb != 0).astype(x.dtype)
            exp_batches = jnp.einsum('nec,nd->ecd', sec_mask, xf)
            h = jax.nn.gelu(jnp.einsum('ecd,edh->ech', exp_batches, c_fc), approximate=False)
            exp_out = jnp.einsum('ech,ehd->ecd', h, c_proj)
            out = jnp.einsum('nec,ecd->nd', cb, exp_out)
            return out.reshape(B, T, D)
        key = jax.random.key(seed)
        k1, k2, k3, k4 = jax.random.split(key, 4)
        B, T, D = (4, 128, 256)
        H = 4 * D
        x = jax.random.normal(k1, (B, T, D), jnp.float32)
        w_g = jax.random.normal(k2, (D, N_EXP), jnp.float32) * 0.02
        c_fc = jax.random.normal(k3, (N_EXP, D, H), jnp.float32) * 0.02
        c_proj = jax.random.normal(k4, (N_EXP, H, D), jnp.float32) * 0.02
        return {'x': x, 'w_g': w_g, 'c_fc': c_fc, 'c_proj': c_proj}
    _L0_ffn_all = _L0_ffn_setup()
    _L0_ffn_in = {k: v for k, v in _L0_ffn_all.items() if k in ('w_g', 'c_fc', 'c_proj')}
    del _L0_ffn_all
    return {'x': x, 'x_txt': x_txt, 'L0_tok_Wq_w': _L0_tok_in['Wq_w'], 'L0_tok_Wq_b': _L0_tok_in['Wq_b'], 'L0_tok_Wk_w': _L0_tok_in['Wk_w'], 'L0_tok_Wk_b': _L0_tok_in['Wk_b'], 'L0_tok_Wv_w': _L0_tok_in['Wv_w'], 'L0_tok_Wv_b': _L0_tok_in['Wv_b'], 'L0_tok_w_bias': _L0_tok_in['w_bias'], 'L0_tok_out_w': _L0_tok_in['out_w'], 'L0_tok_out_b': _L0_tok_in['out_b'], 'L0_tok_ln_g': _L0_tok_in['ln_g'], 'L0_tok_ln_b': _L0_tok_in['ln_b'], 'L0_tok_local_mask': _L0_tok_in['local_mask'], 'L0_txt_emb': _L0_txt_in['emb'], 'L0_txt_Wq': _L0_txt_in['Wq'], 'L0_txt_Wk': _L0_txt_in['Wk'], 'L0_txt_Wv': _L0_txt_in['Wv'], 'L0_txt_Wc': _L0_txt_in['Wc'], 'L0_txt_W1': _L0_txt_in['W1'], 'L0_txt_b1': _L0_txt_in['b1'], 'L0_txt_W2': _L0_txt_in['W2'], 'L0_txt_b2': _L0_txt_in['b2'], 'L0_txt_g1': _L0_txt_in['g1'], 'L0_txt_be1': _L0_txt_in['be1'], 'L0_txt_g2': _L0_txt_in['g2'], 'L0_txt_be2': _L0_txt_in['be2'], 'L0_attn_attention_mask': _L0_attn_in['attention_mask'], 'L0_attn_Wq': _L0_attn_in['Wq'], 'L0_attn_bq': _L0_attn_in['bq'], 'L0_attn_Wqa': _L0_attn_in['Wqa'], 'L0_attn_bqa': _L0_attn_in['bqa'], 'L0_attn_Wk': _L0_attn_in['Wk'], 'L0_attn_bk': _L0_attn_in['bk'], 'L0_attn_Wka': _L0_attn_in['Wka'], 'L0_attn_bka': _L0_attn_in['bka'], 'L0_attn_Wv': _L0_attn_in['Wv'], 'L0_attn_bv': _L0_attn_in['bv'], 'L0_attn_gamma': _L0_attn_in['gamma'], 'L0_attn_beta': _L0_attn_in['beta'], 'L0_ffn_w_g': _L0_ffn_in['w_g'], 'L0_ffn_c_fc': _L0_ffn_in['c_fc'], 'L0_ffn_c_proj': _L0_ffn_in['c_proj']}

def reference(x, x_txt, L0_tok_Wq_w, L0_tok_Wq_b, L0_tok_Wk_w, L0_tok_Wk_b, L0_tok_Wv_w, L0_tok_Wv_b, L0_tok_w_bias, L0_tok_out_w, L0_tok_out_b, L0_tok_ln_g, L0_tok_ln_b, L0_tok_local_mask, L0_txt_emb, L0_txt_Wq, L0_txt_Wk, L0_txt_Wv, L0_txt_Wc, L0_txt_W1, L0_txt_b1, L0_txt_W2, L0_txt_b2, L0_txt_g1, L0_txt_be1, L0_txt_g2, L0_txt_be2, L0_attn_attention_mask, L0_attn_Wq, L0_attn_bq, L0_attn_Wqa, L0_attn_bqa, L0_attn_Wk, L0_attn_bk, L0_attn_Wka, L0_attn_bka, L0_attn_Wv, L0_attn_bv, L0_attn_gamma, L0_attn_beta, L0_ffn_w_g, L0_ffn_c_fc, L0_ffn_c_proj):
    import jax
    import jax.numpy as jnp

    def _L0_tok_ref(x, Wq_w, Wq_b, Wk_w, Wk_b, Wv_w, Wv_b, w_bias, out_w, out_b, ln_g, ln_b, local_mask):
        import jax, jax.numpy as jnp
        import numpy as np
        B, F, L, H, D = (8, 64, 256, 4, 64)
        MODEL = H * F
        WIN = 128

        def _local_mask():
            m = np.ones((L, L), dtype=bool)
            m = np.tril(m, WIN - 1)
            m = np.triu(m, -(WIN - 1))
            return jnp.asarray(m)

        def _flatten(y):
            n = y.shape[0]
            return y.transpose(0, 2, 3, 1).reshape(n, L, -1)

        def proj(w, b):
            y = jnp.einsum('nclh,dc->ndlh', x, w) + b[None, :, None, None]
            return _flatten(y)
        q = proj(Wq_w, Wq_b)
        k = proj(Wk_w, Wk_b)
        v = proj(Wv_w, Wv_b)
        wb = w_bias * local_mask.astype(w_bias.dtype)
        ew = jnp.exp(wb)
        ek = jnp.exp(k)
        num = jnp.einsum('ts,nsd->ntd', ew, ek * v)
        den = jnp.einsum('ts,nsd->ntd', ew, ek)
        y = jax.nn.sigmoid(q) * num / den
        h = y @ out_w + out_b + _flatten(x)
        mu = jnp.mean(h, axis=-1, keepdims=True)
        var = jnp.mean(jnp.square(h - mu), axis=-1, keepdims=True)
        return (h - mu) * jax.lax.rsqrt(var + 1e-05) * ln_g + ln_b

    def _L0_txt_ref(x, emb, Wq, Wk, Wv, Wc, W1, b1, W2, b2, g1, be1, g2, be2):
        import jax, jax.numpy as jnp
        import numpy as np
        VOCAB, D, H, M, L, NMAX = (8000, 256, 16, 1024, 4, 256)
        KD = D // H
        EPS = 1e-05

        def positional_encoding(n, d):
            pos = jnp.arange(n, dtype=jnp.float32)[:, None]
            div = jnp.exp(jnp.arange(0, d, 2, dtype=jnp.float32) * (-jnp.log(10000.0) / d))
            ang = pos * div
            enc = jnp.zeros((n, d), dtype=jnp.float32)
            enc = enc.at[:, 0::2].set(jnp.sin(ang))
            enc = enc.at[:, 1::2].set(jnp.cos(ang))
            return enc

        def _layernorm(z, g, b):
            mu = jnp.mean(z, axis=-1, keepdims=True)
            var = jnp.mean((z - mu) ** 2, axis=-1, keepdims=True)
            return (z - mu) * jax.lax.rsqrt(var + EPS) * g + b

        def _block(h, p):
            wq, wk, wv, wc, w1, bb1, w2, bb2, gg1, e1, gg2, e2 = p
            B, n, d = h.shape

            def heads(w):
                return (h @ w).reshape(B, n, H, KD).transpose(0, 2, 1, 3)
            Q, K, V = (heads(wq), heads(wk), heads(wv))
            scores = jnp.einsum('bhqk,bhlk->bhql', Q, K) / np.sqrt(KD).astype(np.float32)
            attn = jax.nn.softmax(scores, axis=-1)
            out = jnp.einsum('bhql,bhlv->bhqv', attn, V)
            out = out.transpose(0, 2, 1, 3).reshape(B, n, d) @ wc
            h = _layernorm(h + out, gg1, e1)
            ff = jax.nn.relu(h @ w1 + bb1) @ w2 + bb2
            return _layernorm(h + ff, gg2, e2)
        B, n = x.shape
        h = emb[x] + positional_encoding(n, D)[None]

        def step(h, p):
            return (_block(h, p), None)
        h, _ = jax.lax.scan(step, h, (Wq, Wk, Wv, Wc, W1, b1, W2, b2, g1, be1, g2, be2))
        return h

    def _L0_attn_ref(hidden_states, attention_mask, Wq, bq, Wqa, bqa, Wk, bk, Wka, bka, Wv, bv, gamma, beta):
        import jax, jax.numpy as jnp
        import numpy as np
        D = 256

        def _layernorm(x, gamma, beta, eps=1e-05):
            mu = jnp.mean(x, axis=-1, keepdims=True)
            var = jnp.var(x, axis=-1, keepdims=True)
            return (x - mu) * jax.lax.rsqrt(var + eps) * gamma + beta
        h = _layernorm(hidden_states, gamma, beta)
        B, S, d_model = h.shape
        inv_sqrt_d = 1.0 / jnp.sqrt(jnp.float32(d_model))
        query = h @ Wq + bq
        keys = h @ Wk + bk
        values = h @ Wv + bv
        scaling = jnp.arange(1, S + 1, dtype=h.dtype).reshape(1, S, 1)
        query_weight = jax.nn.softmax((query @ Wqa + bqa) * inv_sqrt_d, axis=-1)
        pooled_query = jnp.cumsum(query_weight * query, axis=1) / scaling
        mixed_keys = pooled_query * keys
        keys_weight = jax.nn.softmax((mixed_keys @ Wka + bka) * inv_sqrt_d, axis=-1)
        pooled_keys = jnp.cumsum(keys_weight * mixed_keys, axis=1) / scaling
        return pooled_keys * values

    def _L0_ffn_ref(x, w_g, c_fc, c_proj):
        import jax, jax.numpy as jnp
        import numpy as np
        N_EXP = 8
        TOP_K = 2
        CAP_FACTOR = 1.25
        NEG_INF = -1000000000.0

        def _moe_forward(x, w_g, c_fc, c_proj):
            B, T, D = x.shape
            N = B * T
            xf = x.reshape(N, D)
            logits = xf @ w_g
            topv, topi = jax.lax.top_k(logits, TOP_K)
            full = jnp.full_like(logits, NEG_INF)
            full = full.at[jnp.arange(N)[:, None], topi].set(topv)
            probs = jax.nn.softmax(full, axis=-1)
            capacity = int(TOP_K * CAP_FACTOR * N / N_EXP)
            capacity += capacity % 2
            mask = jax.nn.one_hot(jnp.swapaxes(topi, 0, 1), N_EXP, dtype=jnp.int32)
            rank = jnp.cumsum(mask.reshape(TOP_K * N, N_EXP), axis=0).reshape(TOP_K, N, N_EXP) - 1
            mask = mask * (rank < capacity)
            rank_sel = jnp.sum(mask * rank, axis=-1)
            wts = jnp.sum(mask * probs[None], axis=-1)
            cb = jnp.zeros((N, N_EXP, capacity), x.dtype)
            tok = jnp.arange(N)
            for k in range(TOP_K):
                cb = cb.at[tok, topi[:, k], rank_sel[k]].add(wts[k])
            sec_mask = (cb != 0).astype(x.dtype)
            exp_batches = jnp.einsum('nec,nd->ecd', sec_mask, xf)
            h = jax.nn.gelu(jnp.einsum('ecd,edh->ech', exp_batches, c_fc), approximate=False)
            exp_out = jnp.einsum('ech,ehd->ecd', h, c_proj)
            out = jnp.einsum('nec,ecd->nd', cb, exp_out)
            return out.reshape(B, T, D)
        return _moe_forward(x, w_g, c_fc, c_proj)
    h = _L0_tok_ref(x, L0_tok_Wq_w, L0_tok_Wq_b, L0_tok_Wk_w, L0_tok_Wk_b, L0_tok_Wv_w, L0_tok_Wv_b, L0_tok_w_bias, L0_tok_out_w, L0_tok_out_b, L0_tok_ln_g, L0_tok_ln_b, L0_tok_local_mask)
    h = jnp.concatenate([h, _L0_txt_ref(x_txt, L0_txt_emb, L0_txt_Wq, L0_txt_Wk, L0_txt_Wv, L0_txt_Wc, L0_txt_W1, L0_txt_b1, L0_txt_W2, L0_txt_b2, L0_txt_g1, L0_txt_be1, L0_txt_g2, L0_txt_be2)], axis=1)
    h = h + _L0_attn_ref(_layernorm(h, axis=-1), L0_attn_attention_mask, L0_attn_Wq, L0_attn_bq, L0_attn_Wqa, L0_attn_bqa, L0_attn_Wk, L0_attn_bk, L0_attn_Wka, L0_attn_bka, L0_attn_Wv, L0_attn_bv, L0_attn_gamma, L0_attn_beta)
    h = h + _L0_ffn_ref(_layernorm(h, axis=-1), L0_ffn_w_g, L0_ffn_c_fc, L0_ffn_c_proj)
    return h

_drawn_inputs = setup_inputs


def setup_inputs(seed=0):
    import zlib

    import numpy as np

    out = dict(_drawn_inputs(seed))
    spreads = {'L0_tok_Wq_b': (0.0, 2.0),
     'L0_tok_Wk_b': (0.0, 2.0),
     'L0_tok_Wv_b': (0.0, 0.1),
     'L0_tok_out_b': (0.0, 0.1),
     'L0_tok_ln_g': (1.0, 0.2),
     'L0_tok_ln_b': (0.0, 0.1),
     'L0_txt_b1': (0.0, 0.541),
     'L0_txt_b2': (0.0, 0.446),
     'L0_txt_g1': (1.0, 0.2),
     'L0_txt_be1': (0.0, 0.432),
     'L0_txt_g2': (1.0, 0.6),
     'L0_txt_be2': (0.0, 0.581),
     'L0_attn_bq': (0.0, 2.0),
     'L0_attn_Wqa': (0.0, 2.0),
     'L0_attn_bqa': (1.0, 0.6),
     'L0_attn_bk': (0.0, 2.0),
     'L0_attn_Wka': (0.0, 0.8),
     'L0_attn_bka': (1.0, 0.6),
     'L0_attn_bv': (0.0, 2.0),
     'L0_attn_gamma': (1.0, 0.6),
     'L0_attn_beta': (0.0, 2.0)}
    factors = {'L0_tok_w_bias': 21.517,
     'L0_txt_emb': 22.234,
     'L0_txt_Wq': 47.301,
     'L0_txt_Wk': 42.445,
     'L0_attn_Wq': 64.0,
     'L0_attn_Wk': 64.0,
     'L0_attn_Wv': 64.0,
     'L0_txt_Wv': 3.764,
     'L0_txt_Wc': 3.006,
     'L0_txt_W1': 2.909,
     'L0_ffn_w_g': 8.0,
     'L0_ffn_c_fc': 8.0,
     'L0_ffn_c_proj': 8.0}
    for name, (base, spread) in spreads.items():
        noise = np.random.default_rng([zlib.crc32(name.encode()), seed]).standard_normal(out[name].shape)
        drawn = base * np.exp(spread * noise) if base else spread * noise
        out[name] = jnp.asarray(drawn.astype(out[name].dtype))
    for name, factor in factors.items():
        out[name] = (out[name] * factor).astype(out[name].dtype)
    return out
```

```python
import concourse.bass as bass
from concourse import mybir
from contextlib import ExitStack

F32 = mybir.dt.float32
I32 = mybir.dt.int32
U32 = mybir.dt.uint32
U8 = mybir.dt.uint8
ACT = mybir.ActivationFunctionType
ALU = mybir.AluOpType
AX = mybir.AxisListType

P = 128
B, F, L_TOK, HT = 8, 64, 256, 4
D = 256
DC = D // P
L_TXT = 128
VOCAB, H, KD, M, LAYERS = 8000, 16, 16, 1024, 4
MC = M // P
TPB = (L_TOK + L_TXT) // P
NT = B * TPB
E, TOPK = 8, 2
N = NT * P
CAP = int(TOPK * 1.25 * N / E)
CAP += CAP % 2
SLOTS = E * CAP
CT = 120
CTN = CAP // CT
HALF = CAP // 2
EPS = 1e-5
START = 64

C_ID, C_TRI, C_STRI, C_ONE = 0, 128, 256, 384
C_EO, C_INV, C_IOTA, C_E960, C_NHALF = 512, 514, 517, 525, 533
C_TRASH = 534
C_PE = C_TRASH + TOPK * NT
C_ALL = C_PE + D


class Chain:

    def __init__(self, eng, sem):
        self.eng, self.sem, self.base, self.n = eng, sem, START, 0

    def begin(self, done):
        self.base, self.n = START + done, 0

    def link(self, ins):
        self.n += 1
        ins.then_inc(self.sem, 1)
        self.eng.wait_ge(self.sem, self.base + self.n)

    def end(self, per):
        assert self.n == per, self.n


def program(nc, a, out):
    with ExitStack() as ctx:
        def sb(name, shape, dt=F32):
            return ctx.enter_context(nc.sbuf_tensor(name, shape, dt))

        sems = []

        def sem(name):
            s = ctx.enter_context(nc.semaphore(name))
            if not name.startswith("sw_"):
                sems.append(s)
            return s

        K = sb("consts", [P, C_ALL])
        ident = K[:, C_ID:C_ID + P]
        tri = K[:, C_TRI:C_TRI + P]
        stri = K[:, C_STRI:C_STRI + P]
        ones = K[:, C_ONE:C_ONE + P]
        Hs = sb("hidden", [P, NT, D])
        ps = ctx.enter_context(nc.psum_tensor("banks", [P, 8, 512], F32))
        s = dict(nc=nc, a=a, out=out, sem=sem, K=K, ident=ident, tri=tri, stri=stri, ones=ones, Hs=Hs, ps=ps)
        phases = [tok_phase, txt_phase, attn_phase, router_phase, expert_phase]
        s["xd"] = nc.dram_tensor("dispatched", [SLOTS + TOPK * N, D], F32, kind="Internal").ap()
        s["yd"] = nc.dram_tensor("expert_out", [SLOTS, D], F32, kind="Internal").ap()
        s["scatter_at"] = sb("scatter_at", [P, TOPK * NT], I32)
        s["gather_at"] = sb("gather_at", [P, TOPK * NT], I32)
        s["mix_weights"] = sb("mix_weights", [P, TOPK, NT])
        k_ld = ctx.enter_context(nc.semaphore("consts_loaded"))
        built = []
        for f in phases:
            built.append((f, f(s, None)))
        blk = nc.Block()
        with blk:
            @blk.sync
            def _(sp):
                sp.dma_start(K[:], a["const"]).then_inc(k_ld, 16)
                sp.wait_ge(k_ld, 16)
                for x in sems:
                    sp.sem_inc(x, START)
        for f, made in built:
            with ExitStack() as mem:
                def sbp(name, shape, dt=F32):
                    return mem.enter_context(nc.sbuf_tensor(name, shape, dt))
                s["sb"] = sbp
                f(s, made)


def Hst(Hs, tile, c=None):
    x = Hs[:, bass.ds(tile, 1), :].rearrange("p o d -> p (o d)")
    return x if c is None else x[:, c * P:(c + 1) * P]


def tok_phase(s, made):
    sem = s["sem"]
    if made is None:
        names = ["tw_load", "tw_mask", "tw_exp", "tw_tr", "tw_ready", "x_loaded0", "x_loaded1", "proj_done", "tokact_done", "ekv_done",
                 "mix_done", "y_done", "yt_tr", "yt_done", "o_done", "tvar_done", "trstd_done", "tok_out",
                 "tok_chain", "waited", "tz_scaled"]
        return {n: sem(n) for n in names}
    g = made
    nc, a, K, ident, Hs, ps, sb = s["nc"], s["a"], s["K"], s["ident"], s["Hs"], s["ps"], s["sb"]
    wraw = sb("tok_wraw", [F, 3, F])
    WT = sb("tok_wt", [F + 1, HT, 4 * F])
    wb = sb("tok_wbias", [P, 2, L_TOK])
    msk = sb("tok_mask", [P, 2, L_TOK // 4], I32)
    ewT = sb("tok_ewT", [P, 2, L_TOK])
    ow = sb("tok_outw", [P, DC, D])
    gb = sb("tok_gb", [P, 2, D])
    X1 = sb("tok_x", [F + 1, 2, L_TOK * HT])
    EK = sb("tok_ek", [P, 2, 2, 2 * D])
    EQ = sb("tok_eq", [P, 2, 2, D])
    XR = sb("tok_xr", [P, 2, 2, D])
    DEN = sb("tok_den", [P, 2, D])
    Y = sb("tok_y", [P, 2, D])
    YT = sb("tok_yT", [P, 2, DC, P])
    Z = sb("tok_z", [P, 2, D])
    ST = sb("tok_st", [P, 2, 6])
    MV = sb("tok_mv", [P, 2, 2])
    VE = sb("tok_ve", [P, 2])
    RS = sb("tok_rs", [P, 2])
    x = a["x"].rearrange("n c l h -> n c (l h)")

    blk = nc.Block()
    with blk:
        @blk.sync
        def _(sp):
            for i, n in enumerate(("L0_tok_Wq_w", "L0_tok_Wk_w", "L0_tok_Wv_w")):
                sp.dma_start(wraw[:, i, :], a[n]).then_inc(g["tw_load"], 16)
            sp.dma_start(wb[:], a["L0_tok_w_bias"].rearrange("(c p) s -> p c s", p=P)).then_inc(g["tw_load"], 16)
            sp.dma_start(msk[:], a["L0_tok_local_mask"].rearrange("(c p) s -> p c s", p=P)).then_inc(g["tw_load"], 16)
            sp.dma_start(ow[:], a["L0_tok_out_w"].rearrange("(c p) n -> p c n", p=P)).then_inc(g["tw_load"], 16)
            sp.dma_start(gb[:, 0, :], a["L0_tok_ln_g"].partition_broadcast(P)).then_inc(g["tw_load"], 16)
            sp.dma_start(gb[:, 1, :], a["L0_tok_ln_b"].partition_broadcast(P)).then_inc(g["tw_load"], 16)
            for h in range(HT):
                for i, n in enumerate(("L0_tok_Wq_b", "L0_tok_Wk_b", "L0_tok_Wv_b")):
                    sp.dma_start(WT[F:F + 1, h, i * F:(i + 1) * F], a[n].rearrange("(o n) -> o n", o=1)).then_inc(g["tw_load"], 16)
                sp.dma_start(WT[F:F + 1, h, 3 * F:], a["L0_tok_out_b"][h * F:(h + 1) * F].rearrange("(o n) -> o n", o=1)).then_inc(g["tw_load"], 16)
            with sp.Fori(0, B // 2) as tp:
                for u in range(2):
                    t = tp * 2 + u
                    sp.wait_ge(g["proj_done"], START + 2 * t - 2)
                    sp.dma_start(X1[0:F, u, :], x[bass.ds(t, 1), :, :].rearrange("o c n -> (o c) n")).then_inc(g[f"x_loaded{u}"], 16)

        @blk.gpsimd
        def _(pool):
            pool.memset(X1[F:F + 1, :, :], 1.0).then_inc(g["tw_ready"], 1)
            with pool.Fori(0, B) as t:
                pool.wait_ge(g["tvar_done"], START + t + 1)
                nc.gpsimd.tensor_tensor(out=RS[:], in0=VE[:], in1=K[:, C_NHALF:C_NHALF + 1].to_broadcast([P, 2]), op=ALU.pow).then_inc(g["trstd_done"], 1)

        @blk.tensor
        def _(pe):
            pe.wait_ge(g["tw_load"], START + 16 * 24)
            for i in range(3):
                last = nc.tensor.transpose(ps[0:F, 0, i * F:(i + 1) * F], wraw[:, i, :], ident[0:F, 0:F])
            last.then_inc(g["tw_tr"], 1)
            pe.wait_ge(g["tw_exp"], START + 1)
            for sc in range(2):
                for tc in range(2):
                    last = nc.tensor.transpose(ps[:, 1, sc * 256 + tc * P:sc * 256 + (tc + 1) * P], wb[:, tc, sc * P:(sc + 1) * P], ident)
            last.then_inc(g["tw_tr"], 1)
            pe.wait_ge(g["tw_ready"], START + 1 + 6)
            with pe.Fori(0, B // 2) as tp:
                for u in range(2):
                    t = tp * 2 + u
                    pe.wait_ge(g[f"x_loaded{u}"], START + tp * 16 + 16)
                    for lt in range(2):
                        pe.wait_ge(g["ekv_done"], START + 2 * t + lt - 1)
                        xv = X1[:, u, :].rearrange("c (l h) -> c h l", h=HT)
                        for h in range(HT):
                            last = nc.tensor.matmul(ps[:, 2 * lt + h // 2, (h % 2) * 256:(h % 2) * 256 + 256],
                                                    xv[:, h, lt * P:(lt + 1) * P], WT[:, h, :], start=True, stop=True)
                        last.then_inc(g["proj_done"], 1)
                    pe.wait_ge(g["ekv_done"], START + 2 * t + 2)
                    for tt in range(2):
                        pe.wait_ge(g["y_done"], START + 2 * t + tt - 1)
                        for sc in range(2):
                            last = nc.tensor.matmul(ps[:, 4 + tt, :], ewT[:, sc, tt * P:(tt + 1) * P], EK[:, u, sc, :],
                                                    start=(sc == 0), stop=(sc == 1))
                        last.then_inc(g["mix_done"], 1)
                    for tt in range(2):
                        pe.wait_ge(g["y_done"], START + 2 * t + tt + 1)
                        pe.wait_ge(g["yt_done"], START + 2 * t + tt)
                        for c in range(DC):
                            last = nc.tensor.transpose(ps[:, 6, c * P:(c + 1) * P], Y[:, tt, c * P:(c + 1) * P], ident)
                        last.then_inc(g["yt_tr"], 1)
                    for tt in range(2):
                        pe.wait_ge(g["yt_done"], START + 2 * t + tt + 1)
                        pe.wait_ge(g["tz_scaled"], START + 2 * t + tt)
                        for c in range(DC):
                            last = nc.tensor.matmul(ps[:, 7, 0:D], YT[:, tt, c, :], ow[:, c, :], start=(c == 0), stop=(c == DC - 1))
                        last.then_inc(g["o_done"], 1)

        @blk.scalar
        def _(act):
            act.wait_ge(g["tw_mask"], START + 1)
            nc.scalar.activation(wb[:], wb[:], ACT.Exp).then_inc(g["tw_exp"], 1)
            with act.Fori(0, B // 2) as tp:
                for u in range(2):
                    t = tp * 2 + u
                    act.wait_ge(g["mix_done"], START + 2 * t - 2)
                    act.wait_ge(g["tok_out"], START + 2 * t - 2)
                    for lt in range(2):
                        act.wait_ge(g["proj_done"], START + 2 * t + lt + 1)
                        v = ps[:, 2 * lt:2 * lt + 2, :].rearrange("p b (h f) -> p (b h) f", f=256)
                        nc.scalar.activation(EK[:, u, lt, D:2 * D].rearrange("p (h f) -> p h f", f=F), v[:, :, F:2 * F], ACT.Exp)
                        nc.scalar.activation(EQ[:, u, lt, :].rearrange("p (h f) -> p h f", f=F), v[:, :, 0:F], ACT.Exp, scale=-1.0)
                        nc.scalar.activation(XR[:, u, lt, :].rearrange("p (h f) -> p h f", f=F), v[:, :, 3 * F:4 * F], ACT.Copy).then_inc(g["tokact_done"], 1)
                    for tt in range(2):
                        act.wait_ge(g["yt_tr"], START + 2 * t + tt + 1)
                        nc.scalar.activation(YT[:, tt, :, :].rearrange("p c n -> p (c n)"), ps[:, 6, 0:D], ACT.Copy).then_inc(g["yt_done"], 1)

        @blk.vector
        def _(dve):
            ch = Chain(dve, g["tok_chain"])
            dve.wait_ge(g["tw_load"], START + 16 * 24)
            nc.vector.tensor_tensor(out=wb[:], in0=wb[:], in1=msk[:].bitcast(U8), op=ALU.mult).then_inc(g["tw_mask"], 1)
            dve.wait_ge(g["tw_tr"], START + 1)
            for h in range(HT):
                nc.vector.tensor_copy(WT[0:F, h, 0:3 * F], ps[0:F, 0, 0:3 * F]).then_inc(g["tw_ready"], 1)
            nc.vector.tensor_copy(WT[0:F, :, 3 * F:], ident[0:F, None, 0:F].to_broadcast([F, HT, F])).then_inc(g["tw_ready"], 1)
            dve.wait_ge(g["tw_tr"], START + 2)
            nc.vector.tensor_copy(ewT[:].rearrange("p c n -> p (c n)"), ps[:, 1, :]).then_inc(g["tw_ready"], 1)
            PER = 14
            with dve.Fori(0, B // 2) as tp:
                for u in range(2):
                    t = tp * 2 + u
                    ch.begin(t * PER)
                    for lt in range(2):
                        dve.wait_ge(g["tokact_done"], START + 2 * t + lt + 1)
                        v = ps[:, 2 * lt:2 * lt + 2, :].rearrange("p b (h f) -> p (b h) f", f=256)
                        nc.vector.tensor_tensor(out=EK[:, u, lt, 0:D].rearrange("p (h f) -> p h f", f=F), in0=v[:, :, 2 * F:3 * F],
                                                in1=EK[:, u, lt, D:2 * D].rearrange("p (h f) -> p h f", f=F), op=ALU.mult).then_inc(g["ekv_done"], 1)
                    for tt in range(2):
                        dve.wait_ge(g["mix_done"], START + 2 * t + tt + 1)
                        ch.link(nc.vector.scalar_tensor_tensor(out=DEN[:, tt, :], in0=EQ[:, u, tt, :], scalar=1.0, in1=ps[:, 4 + tt, D:2 * D], op0=ALU.add, op1=ALU.mult))
                        ch.link(nc.vector.reciprocal(DEN[:, tt, :], DEN[:, tt, :]))
                        nc.vector.tensor_tensor(out=Y[:, tt, :], in0=ps[:, 4 + tt, 0:D], in1=DEN[:, tt, :], op=ALU.mult).then_inc(g["y_done"], 1)
                    for tt in range(2):
                        dve.wait_ge(g["o_done"], START + 2 * t + tt + 1)
                        nc.vector.tensor_tensor(out=Z[:, tt, :], in0=ps[:, 7, 0:D], in1=XR[:, u, tt, :], op=ALU.add).then_inc(g["tz_scaled"], 1)
                        dve.wait_ge(g["tz_scaled"], START + 2 * t + tt + 1)
                        ch.link(nc.vector.bn_stats(ST[:, tt, :], Z[:, tt, :]))
                        dve.sem_inc(g["waited"], 1)
                        ch.link(nc.vector.bn_aggr(MV[:, tt, :], ST[:, tt, :]))
                    nc.vector.tensor_scalar(out=VE[:], in0=MV[:, :, 1], scalar1=EPS, scalar2=None, op0=ALU.add).then_inc(g["tvar_done"], 1)
                    dve.wait_ge(g["trstd_done"], START + t + 1)
                    for tt in range(2):
                        ch.link(nc.vector.tensor_scalar(out=Z[:, tt, :], in0=Z[:, tt, :], scalar1=MV[:, tt, 0:1], scalar2=RS[:, tt:tt + 1], op0=ALU.subtract, op1=ALU.mult))
                        ch.link(nc.vector.tensor_tensor(out=Z[:, tt, :], in0=Z[:, tt, :], in1=gb[:, 0, :], op=ALU.mult))
                        ch.link(nc.vector.tensor_tensor(out=Hs[:, bass.ds(t * TPB + tt, 1), :].rearrange("p o d -> p (o d)"), in0=Z[:, tt, :], in1=gb[:, 1, :], op=ALU.add))
                        nc.vector.sem_inc(g["tok_out"], 1)
                    ch.end(PER)


def txt_phase(s, made):
    sem = s["sem"]
    if made is None:
        names = ["ids_loaded", "ids_chain", "ids_ready", "sw_emb", "emb_ready", "v_ones", "w_loaded0", "w_loaded1", "h_tr", "ht_act", "ht_dve",
                 "qk_mm", "v_mm", "q_done", "k_done", "v_done", "s_done", "max_done", "exp_done", "pt_tr", "pt_done", "pv_done",
                 "onorm_done", "ot_tr", "ot_done", "wc_done", "z1_done", "var1_done", "rstd1_done", "h1_done", "h1b_done",
                 "h1_tr", "h1t_act", "h1t_dve", "ff1_mm", "ff1_done", "ff2_done", "z2_done", "var2_done", "rstd2_done", "txt_out",
                 "txt_chain", "txt_waited"]
        return {n: sem(n) for n in names}
    g = made
    nc, a, K, ident, Hs, ps, sb = s["nc"], s["a"], s["K"], s["ident"], s["Hs"], s["ps"], s["sb"]
    G = 4
    ids = sb("ids", [P, B], I32)
    idf = sb("ids_f", [P, B])
    idn = sb("ids_neg", [P, B])
    W = []
    for p in range(2):
        W.append(dict(qkv=sb(f"w_qkv{p}", [P, DC, 3, D]), wc=sb(f"w_c{p}", [P, DC, D]), w1=sb(f"w_1{p}", [P, DC, M]),
                      w2=sb(f"w_2{p}", [P, MC, D]), vec=sb(f"w_vec{p}", [P, 5, D]), b1=sb(f"w_b1{p}", [P, MC])))
    hT = sb("hT", [P, DC, G * P])
    QT = sb("qT", [P, DC, G * P])
    K2 = sb("kT_masked", [P, DC, G, 2, P])
    V1 = sb("v_ones", [P, G, H, KD + 1])
    PR = sb("probs", [P, 4, 4, P])
    NM = sb("neg_max", [P, 4, 4])
    PT = sb("probsT", [P, 2, 4, P])
    RC = sb("recip", [P, H])
    O = sb("heads_out", [P, D])
    OT = sb("heads_outT", [P, DC, P])
    Z = sb("z1", [P, G, D])
    Z2 = sb("z2", [P, G, D])
    H1B = sb("h1_b2", [P, G, D])
    F1T = sb("ff1T", [P, MC, G * P])
    ST = sb("txt_st", [P, G, 6])
    MV = sb("txt_mv", [P, G, 2])
    VE = sb("txt_ve", [P, G])
    RS = sb("txt_rs", [P, G])
    h1T = hT

    def heads_of(bank, slot):
        return (slot // 2) * 8 + bank * 2 + slot % 2

    blk = nc.Block()
    with blk:
        @blk.sync
        def _(sp):
            sp.dma_start(ids[:], a["x_txt"].rearrange("b n -> n b"), allow_slow_non_contiguous=True).then_inc(g["ids_loaded"], 16)
            with sp.Fori(0, LAYERS // 2) as lp:
                for p in range(2):
                    w, done = W[p], g[f"w_loaded{p}"]
                    lay = lp * 2 + p
                    sp.wait_ge(g["txt_out"], START + B * lay - B)

                    def at(n):
                        return a["L0_txt_" + n]
                    for i, n in enumerate(("Wq", "Wk", "Wv")):
                        sp.dma_start(w["qkv"][:, :, i, :], at(n)[bass.ds(lay, 1)].rearrange("o (c p) n -> p (o c) n", p=P)).then_inc(done, 16)
                    sp.dma_start(w["wc"][:], at("Wc")[bass.ds(lay, 1)].rearrange("o (c p) n -> p (o c) n", p=P)).then_inc(done, 16)
                    sp.dma_start(w["w1"][:], at("W1")[bass.ds(lay, 1)].rearrange("o (c p) n -> p (o c) n", p=P)).then_inc(done, 16)
                    sp.dma_start(w["w2"][:], at("W2")[bass.ds(lay, 1)].rearrange("o (c p) n -> p (o c) n", p=P)).then_inc(done, 16)
                    for i, n in enumerate(("b2", "g1", "be1", "g2", "be2")):
                        sp.dma_start(w["vec"][:, i, :], at(n)[bass.ds(lay, 1), :].to_broadcast([P, D])).then_inc(done, 16)
                    sp.dma_start(w["b1"][:], at("b1")[bass.ds(lay, 1), :].rearrange("o (c p) -> p (o c)", p=P), allow_slow_non_contiguous=True).then_inc(done, 16)

        @blk.gpsimd
        def _(pool):
            pool.memset(V1[:, :, :, KD:KD + 1], 1.0).then_inc(g["v_ones"], 1)
            pool.wait_ge(g["ids_ready"], START + 1)
            for b in range(B):
                pool.indirect_dma_start(out=Hs[:, b * TPB + 2, :], out_offset=None, in_=a["L0_txt_emb"],
                                        in_offset=bass.IndirectOffsetOnAxis(ap=ids[:, b:b + 1], axis=0)).then_inc(g["sw_emb"], 16)
            with pool.Fori(0, LAYERS // 2) as lp:
                for p in range(2):
                    pool.wait_ge(g[f"w_loaded{p}"], START + 192 * lp + 192)
                    for hf in range(2):
                        q = lp * 4 + p * 2 + hf
                        half = K[:, C_NHALF:C_NHALF + 1].to_broadcast([P, G])
                        pool.wait_ge(g["var1_done"], START + q + 1)
                        nc.gpsimd.tensor_tensor(out=RS[:], in0=VE[:], in1=half, op=ALU.pow).then_inc(g["rstd1_done"], 1)
                        pool.wait_ge(g["z2_done"], START + q * G)
                        for j in range(G):
                            pool.wait_ge(g["h1_done"], START + q * G + j + 1)
                            nc.gpsimd.tensor_tensor(out=H1B[:, j, :], in0=Z[:, j, :], in1=W[p]["vec"][:, 0, :], op=ALU.add).then_inc(g["h1b_done"], 1)
                        pool.wait_ge(g["var2_done"], START + q + 1)
                        nc.gpsimd.tensor_tensor(out=RS[:], in0=VE[:], in1=half, op=ALU.pow).then_inc(g["rstd2_done"], 1)

        @blk.tensor
        def _(pe):
            pe.wait_ge(g["emb_ready"], START + 1)
            pe.wait_ge(g["v_ones"], START + 1)
            with pe.Fori(0, LAYERS // 2) as lp:
                for p in range(2):
                    w = W[p]
                    pe.wait_ge(g[f"w_loaded{p}"], START + 192 * lp + 192)
                    for hf in range(2):
                        q = lp * 4 + p * 2 + hf
                        T = q * G

                        def transpose_group(name, src, count):
                            for c in range(DC):
                                for j in range(G):
                                    if c == 0:
                                        pe.wait_ge(g[count], START + T + j + 1)
                                    last = nc.tensor.transpose(ps[:, 4 + c, j * P:(j + 1) * P], src(j, c), ident)
                                last.then_inc(g[name], 1)

                        pe.wait_ge(g["txt_out"], START + T - G)
                        pe.wait_ge(g["h1t_act"], START + q)
                        pe.wait_ge(g["h1t_dve"], START + q)
                        for c in range(DC):
                            for j in range(G):
                                tile = hf * (G * TPB) + (j * TPB + 2)
                                last = nc.tensor.transpose(ps[:, 4 + c, j * P:(j + 1) * P],
                                                           Hst(Hs, tile, c), ident)
                            last.then_inc(g["h_tr"], 1)
                        pe.wait_ge(g["ht_act"], START + q + 1)
                        pe.wait_ge(g["ht_dve"], START + q + 1)
                        for i in range(2):
                            for dc in range(DC):
                                for c in range(DC):
                                    last = nc.tensor.matmul(ps[:, 2 * i + dc, :], w["qkv"][:, c, i, dc * P:(dc + 1) * P], hT[:, c, :],
                                                            start=(c == 0), stop=(c == DC - 1))
                                last.then_inc(g["qk_mm"], 1)
                        pe.wait_ge(g["z2_done"], START + T)
                        for j in range(G):
                            for c in range(DC):
                                last = nc.tensor.matmul(ps[:, 6 + j // 2, (j % 2) * D:(j % 2) * D + D], hT[:, c, j * P:(j + 1) * P], w["qkv"][:, c, 2, :],
                                                        start=(c == 0), stop=(c == DC - 1))
                            last.then_inc(g["v_mm"], 1)
                        pe.wait_ge(g["q_done"], START + 2 * q + 2)
                        pe.wait_ge(g["k_done"], START + 2 * q + 2)

                        def scores(j, b):
                            n = T * 4 + (4 * j + b)
                            if j > 0:
                                pe.wait_ge(g["exp_done"], START + n - 3)
                            for c in range(DC):
                                last = nc.tensor.matmul(ps[:, b, c * 256:(c + 1) * 256], QT[32 * b:32 * b + 32, c, j * P:(j + 1) * P],
                                                        K2[32 * b:32 * b + 32, c, j, :, :].rearrange("p e l -> p (e l)"), start=True, stop=True)
                            last.then_inc(g["s_done"], 1)

                        def probs_transpose(j, b):
                            n = T * 4 + (4 * j + b)
                            pe.wait_ge(g["exp_done"], START + n + 1)
                            pe.wait_ge(g["pt_done"], START + n - 1)
                            for i in range(4):
                                last = nc.tensor.transpose(ps[:, 4 + b % 2, i * P:(i + 1) * P], PR[:, b, i, :], ident)
                            last.then_inc(g["pt_tr"], 1)

                        def values(j, b):
                            n = T * 4 + (4 * j + b)
                            pe.wait_ge(g["pt_done"], START + n + 1)
                            if b == 0:
                                pe.wait_ge(g["v_done"], START + T + 4)
                                pe.wait_ge(g["onorm_done"], START + T + j)
                            for i in range(4):
                                h = heads_of(b, i)
                                last = nc.tensor.matmul(ps[:, 6, h * (KD + 1):(h + 1) * (KD + 1)], PT[:, b % 2, i, :], V1[:, j, h, :], start=True, stop=True)
                            last.then_inc(g["pv_done"], 1)

                        def out_transpose(j):
                            pe.wait_ge(g["onorm_done"], START + T + j + 1)
                            pe.wait_ge(g["z1_done"], START + T + j)
                            for c in range(DC):
                                last = nc.tensor.transpose(ps[:, 7, c * P:(c + 1) * P], O[:, c * P:(c + 1) * P], ident)
                            last.then_inc(g["ot_tr"], 1)

                        def out_project(j):
                            pe.wait_ge(g["ot_done"], START + T + j + 1)
                            for c in range(DC):
                                last = nc.tensor.matmul(ps[:, 7, D:2 * D], OT[:, c, :], w["wc"][:, c, :], start=(c == 0), stop=(c == DC - 1))
                            last.then_inc(g["wc_done"], 1)

                        for b in range(4):
                            scores(0, b)
                        for j in range(G):
                            for b in range(4):
                                if j + 1 < G:
                                    scores(j + 1, b)
                                probs_transpose(j, b)
                                if b > 0:
                                    values(j, b - 1)
                                if j > 0 and b == 1:
                                    out_transpose(j - 1)
                                if j > 0 and b == 3:
                                    out_project(j - 1)
                            values(j, 3)
                        out_transpose(G - 1)
                        out_project(G - 1)

                        transpose_group("h1_tr", lambda j, c: Z[:, j, c * P:(c + 1) * P], "h1_done")
                        pe.wait_ge(g["h1t_act"], START + q + 1)
                        pe.wait_ge(g["h1t_dve"], START + q + 1)
                        for m in range(MC):
                            pe.wait_ge(g["ff1_done"], START + q * MC + m - 3)
                            for c in range(DC):
                                last = nc.tensor.matmul(ps[:, m % 4, :], w["w1"][:, c, m * P:(m + 1) * P], h1T[:, c, :], start=(c == 0), stop=(c == DC - 1))
                            last.then_inc(g["ff1_mm"], 1)
                        pe.wait_ge(g["ff1_done"], START + q * MC + MC)
                        for j in range(G):
                            pe.wait_ge(g["z2_done"], START + T + j - 1)
                            for m in range(MC):
                                last = nc.tensor.matmul(ps[:, 6 + j % 2, 0:D], F1T[:, m, j * P:(j + 1) * P], w["w2"][:, m, :], start=(m == 0), stop=(m == MC - 1))
                            last.then_inc(g["ff2_done"], 1)

        @blk.scalar
        def _(act):
            with act.Fori(0, LAYERS // 2) as lp:
                for p in range(2):
                    w = W[p]
                    act.wait_ge(g[f"w_loaded{p}"], START + 192 * lp + 192)
                    for hf in range(2):
                        q = lp * 4 + p * 2 + hf
                        T = q * G
                        act.wait_ge(g["h_tr"], START + 2 * q + 1)
                        act.wait_ge(g["ff1_mm"], START + q * MC)
                        nc.scalar.activation(hT[:, 0, :], ps[:, 4, :], ACT.Copy).then_inc(g["ht_act"], 1)
                        for dc in range(DC):
                            act.wait_ge(g["qk_mm"], START + 4 * q + dc + 1)
                            nc.scalar.activation(QT[:, dc, :], ps[:, dc, :], ACT.Copy, scale=float(KD) ** -0.5).then_inc(g["q_done"], 1)
                        for j in range(G):
                            act.wait_ge(g["v_mm"], START + T + (2 * (j // 2) + 2))
                            nc.scalar.activation(V1[:, j, :, 0:KD], ps[:, 6 + j // 2, (j % 2) * D:(j % 2) * D + D].rearrange("p (h k) -> p h k", k=KD), ACT.Copy).then_inc(g["v_done"], 1)

                        def out_copy(j):
                            act.wait_ge(g["ot_tr"], START + T + j + 1)
                            act.wait_ge(g["wc_done"], START + T + j)
                            nc.scalar.activation(OT[:].rearrange("p c n -> p (c n)"), ps[:, 7, 0:D], ACT.Copy).then_inc(g["ot_done"], 1)

                        for j in range(G):
                            for b in range(4):
                                n = T * 4 + (4 * j + b)
                                act.wait_ge(g["max_done"], START + n + 1)
                                act.wait_ge(g["pt_tr"], START + n - 3)
                                for i in range(4):
                                    last = nc.scalar.activation(PR[:, b, i, :], ps[:, b, i * P:(i + 1) * P], ACT.Exp, bias=NM[:, b, i:i + 1])
                                last.then_inc(g["exp_done"], 1)
                                if j > 0 and b == 2:
                                    out_copy(j - 1)
                        out_copy(G - 1)
                        act.wait_ge(g["h1_tr"], START + 2 * q + 1)
                        nc.scalar.activation(h1T[:, 0, :], ps[:, 4, :], ACT.Copy).then_inc(g["h1t_act"], 1)
                        act.wait_ge(g["ff2_done"], START + T)
                        for m in range(MC):
                            act.wait_ge(g["ff1_mm"], START + q * MC + m + 1)
                            nc.scalar.activation(F1T[:, m, :], ps[:, m % 4, :], ACT.Relu, bias=w["b1"][:, m:m + 1]).then_inc(g["ff1_done"], 1)

        @blk.vector
        def _(dve):
            ic = Chain(dve, g["ids_chain"])
            dve.wait_ge(g["ids_loaded"], START + 16)
            ic.link(nc.vector.tensor_copy(idf[:], ids[:]))
            ic.link(nc.vector.tensor_scalar(out=idn[:], in0=idf[:], scalar1=0.0, scalar2=float(VOCAB), op0=ALU.is_lt, op1=ALU.mult))
            ic.link(nc.vector.tensor_tensor(out=idf[:], in0=idf[:], in1=idn[:], op=ALU.add))
            ic.link(nc.vector.tensor_scalar(out=idf[:], in0=idf[:], scalar1=0.0, scalar2=float(VOCAB - 1), op0=ALU.max, op1=ALU.min))
            nc.vector.tensor_copy(ids[:], idf[:]).then_inc(g["ids_ready"], 1)
            dve.wait_ge(g["sw_emb"], 16 * B)
            hv = Hs[:].rearrange("p (b t) d -> p b t d", t=TPB)[:, :, TPB - 1, :]
            nc.vector.tensor_tensor(out=hv, in0=hv, in1=K[:, None, C_PE:C_PE + D].to_broadcast([P, B, D]), op=ALU.add).then_inc(g["emb_ready"], 1)
            ch = Chain(dve, g["txt_chain"])
            PER = 36
            with dve.Fori(0, LAYERS // 2) as lp:
                for p in range(2):
                    w = W[p]
                    b2, g1, be1, g2, be2 = (w["vec"][:, i, :] for i in range(5))
                    dve.wait_ge(g[f"w_loaded{p}"], START + 192 * lp + 192)
                    for hf in range(2):
                        q = lp * 4 + p * 2 + hf
                        T = q * G
                        ch.begin(q * PER)
                        dve.wait_ge(g["h_tr"], START + 2 * q + 2)
                        dve.wait_ge(g["ff1_mm"], START + q * MC)
                        nc.vector.tensor_copy(hT[:, 1, :], ps[:, 5, :]).then_inc(g["ht_dve"], 1)
                        for dc in range(DC):
                            dve.wait_ge(g["qk_mm"], START + 4 * q + (2 + dc + 1))
                            kt = ps[:, 2 + dc, :].rearrange("p (g l) -> p g l", g=G)
                            nc.vector.tensor_scalar(out=K2[:, dc, :, 0, :], in0=kt, scalar1=K[:, C_EO:C_EO + 1], scalar2=None, op0=ALU.mult)
                            nc.vector.tensor_scalar(out=K2[:, dc, :, 1, :], in0=kt, scalar1=K[:, C_EO + 1:C_EO + 2], scalar2=None, op0=ALU.mult).then_inc(g["k_done"], 1)

                        def row_max(j, b):
                            n = T * 4 + (4 * j + b)
                            dve.wait_ge(g["s_done"], START + n + 1)
                            dve.wait_ge(g["exp_done"], START + n - 3)
                            nc.vector.tensor_reduce(out=NM[:, b, :], in_=ps[:, b, :].rearrange("p (i l) -> p i l", i=4), op=ALU.max, axis=AX.X, negate=True).then_inc(g["max_done"], 1)

                        def probs_copy(j, b):
                            n = T * 4 + (4 * j + b)
                            dve.wait_ge(g["pt_tr"], START + n + 1)
                            dve.wait_ge(g["pv_done"], START + n - 1)
                            nc.vector.tensor_copy(PT[:, b % 2, :, :].rearrange("p i l -> p (i l)"), ps[:, 4 + b % 2, :]).then_inc(g["pt_done"], 1)

                        def normalise(j):
                            dve.wait_ge(g["pv_done"], START + T * 4 + 4 * (j + 1))
                            dve.wait_ge(g["ot_tr"], START + T + j)
                            ov = ps[:, 6, 0:H * (KD + 1)].rearrange("p (h k) -> p h k", k=KD + 1)
                            ch.link(nc.vector.reciprocal(RC[:], ov[:, :, KD]))
                            nc.vector.tensor_tensor(out=O[:].rearrange("p (h k) -> p h k", k=KD), in0=ov[:, :, 0:KD],
                                                    in1=RC[:, :, None].to_broadcast([P, H, KD]), op=ALU.mult).then_inc(g["onorm_done"], 1)

                        def stats(z, j):
                            ch.link(nc.vector.bn_stats(ST[:, j, :], z))
                            dve.sem_inc(g["txt_waited"], 1)
                            ch.link(nc.vector.bn_aggr(MV[:, j, :], ST[:, j, :]))

                        def residual1(j):
                            dve.wait_ge(g["wc_done"], START + T + j + 1)
                            tile = hf * (G * TPB) + (j * TPB + 2)
                            nc.vector.tensor_tensor(out=Z[:, j, :], in0=ps[:, 7, D:2 * D], in1=Hst(Hs, tile), op=ALU.add).then_inc(g["z1_done"], 1)
                            dve.wait_ge(g["z1_done"], START + T + j + 1)
                            stats(Z[:, j, :], j)

                        def norm(z, j, ga, be, to, count):
                            ch.link(nc.vector.tensor_scalar(out=z, in0=z, scalar1=MV[:, j, 0:1], scalar2=RS[:, j:j + 1], op0=ALU.subtract, op1=ALU.mult))
                            ch.link(nc.vector.tensor_tensor(out=z, in0=z, in1=ga, op=ALU.mult))
                            nc.vector.tensor_tensor(out=to, in0=z, in1=be, op=ALU.add).then_inc(g[count], 1)

                        dve.wait_ge(g["h1b_done"], START + T)
                        for b in range(4):
                            row_max(0, b)
                        for j in range(G):
                            for b in range(4):
                                if j + 1 < G:
                                    row_max(j + 1, b)
                                probs_copy(j, b)
                                if j > 0 and b == 0:
                                    normalise(j - 1)
                                if j > 1 and b == 0:
                                    residual1(j - 2)
                        normalise(G - 1)
                        residual1(G - 2)
                        residual1(G - 1)
                        nc.vector.tensor_scalar(out=VE[:], in0=MV[:, :, 1], scalar1=EPS, scalar2=None, op0=ALU.add).then_inc(g["var1_done"], 1)
                        dve.wait_ge(g["rstd1_done"], START + q + 1)
                        for j in range(G):
                            norm(Z[:, j, :], j, g1, be1, Z[:, j, :], "h1_done")
                        dve.wait_ge(g["h1_tr"], START + 2 * q + 2)
                        nc.vector.tensor_copy(h1T[:, 1, :], ps[:, 5, :]).then_inc(g["h1t_dve"], 1)
                        for j in range(G):
                            dve.wait_ge(g["ff2_done"], START + T + j + 1)
                            dve.wait_ge(g["h1b_done"], START + T + j + 1)
                            nc.vector.tensor_tensor(out=Z2[:, j, :], in0=ps[:, 6 + j % 2, 0:D], in1=H1B[:, j, :], op=ALU.add).then_inc(g["z2_done"], 1)
                            dve.wait_ge(g["z2_done"], START + T + j + 1)
                            stats(Z2[:, j, :], j)
                        nc.vector.tensor_scalar(out=VE[:], in0=MV[:, :, 1], scalar1=EPS, scalar2=None, op0=ALU.add).then_inc(g["var2_done"], 1)
                        dve.wait_ge(g["rstd2_done"], START + q + 1)
                        for j in range(G):
                            tile = hf * (G * TPB) + (j * TPB + 2)
                            norm(Z2[:, j, :], j, g2, be2, Hst(Hs, tile), "txt_out")
                        ch.end(PER)


def attn_phase(s, made):
    sem = s["sem"]
    if made is None:
        names = ["aw_load", "wqT_tr", "wqT_done", "fold_mm", "aw_ready", "aw_rep", "avar_done", "arstd_done", "u_done", "gt_tr", "gt_done",
                 "aproj_done", "kv_done", "max1_done", "exp1_done", "wq_done", "cum1_done", "m_done", "t2_tr", "mt_done", "klog_done",
                 "kl_done", "max2_done", "exp2_done", "kw_done", "cum2_done", "attn_out", "attn_chain", "attn_waited"]
        return {n: sem(n) for n in names}
    g = made
    nc, a, K, ident, Hs, ps, sb = s["nc"], s["a"], s["K"], s["ident"], s["Hs"], s["ps"], s["sb"]
    tri, ones = s["tri"], s["ones"]
    W = sb("a_w", [P, DC, 4, D])
    WKA = sb("a_wka", [P, DC, D])
    WQA = sb("a_wqa", [P, DC, D])
    WQT = sb("a_wqT", [P, DC, D])
    BI = sb("a_bias", [P, 4, D])
    BKA = sb("a_bka", [P, D])
    COL = sb("a_cols", [P, 3, DC])
    BQR = sb("a_bq_rep", [P, DC, P])
    U = sb("a_u", [P, 2, TPB, D])
    GT = sb("a_gT", [P, TPB, DC, P])
    QA = sb("a_qa", [P, 2, TPB, 2, D])
    KV = sb("a_kv", [P, 2, TPB, 2, D])
    WQ = sb("a_weighted_q", [P, TPB, D])
    Mx = sb("a_mixed", [P, TPB, D])
    MT = sb("a_mixedT", [P, TPB, DC, P])
    KL = sb("a_klog", [P, TPB, D])
    KW = sb("a_weighted_k", [P, TPB, D])
    TM = sb("a_tmp", [P, TPB, D])
    ST = sb("a_st", [P, TPB, 6])
    MV = sb("a_mv", [P, TPB, 2])
    VE = sb("a_ve", [P, TPB])
    RS = sb("a_rs", [P, TPB])
    NM = sb("a_negmax", [P, 2, TPB])
    SM = sb("a_sum", [P, 2, TPB])
    SCALE = float(D) ** -0.5

    def steps(eng, before, body):
        before()
        with eng.Fori(0, B // 2 - 1) as bp:
            for u in range(2):
                body(bp * 2 + u, u, None)
        for b in (B - 2, B - 1):
            body(b, b % 2, b)

    blk = nc.Block()
    with blk:
        @blk.sync
        def _(sp):
            for i, n in ((0, "Wq"), (2, "Wk"), (3, "Wv")):
                sp.dma_start(W[:, :, i, :], a["L0_attn_" + n].rearrange("(c p) n -> p c n", p=P)).then_inc(g["aw_load"], 16)
            sp.dma_start(WQA[:], a["L0_attn_Wqa"].rearrange("(c p) n -> p c n", p=P)).then_inc(g["aw_load"], 16)
            sp.dma_start(WKA[:], a["L0_attn_Wka"].rearrange("(c p) n -> p c n", p=P)).then_inc(g["aw_load"], 16)
            for i, n in enumerate(("bq", "bqa", "bk", "bv")):
                sp.dma_start(BI[:, i, :], a["L0_attn_" + n].partition_broadcast(P)).then_inc(g["aw_load"], 16)
            sp.dma_start(BKA[:], a["L0_attn_bka"].partition_broadcast(P)).then_inc(g["aw_load"], 16)
            for i, n in enumerate(("gamma", "beta", "bq")):
                sp.dma_start(COL[:, i, :], a["L0_attn_" + n].rearrange("(c p) -> p c", p=P), allow_slow_non_contiguous=True).then_inc(g["aw_load"], 16)

        @blk.gpsimd
        def _(pool):
            with pool.Fori(0, B) as b:
                pool.wait_ge(g["avar_done"], START + b + 1)
                nc.gpsimd.tensor_tensor(out=RS[:], in0=VE[:], in1=K[:, C_NHALF:C_NHALF + 1].to_broadcast([P, TPB]), op=ALU.pow).then_inc(g["arstd_done"], 1)

        @blk.tensor
        def _(pe):
            pe.wait_ge(g["aw_load"], START + 16 * 13)
            for mc in range(DC):
                for c in range(DC):
                    last = nc.tensor.transpose(ps[:, 0, mc * D + c * P:mc * D + (c + 1) * P], W[:, c, 0, mc * P:(mc + 1) * P], ident)
            last.then_inc(g["wqT_tr"], 1)
            pe.wait_ge(g["wqT_done"], START + 1)
            for c in range(DC):
                for mc in range(DC):
                    last = nc.tensor.matmul(ps[:, 1, c * D:(c + 1) * D], WQT[:, mc, c * P:(c + 1) * P], WQA[:, mc, :], start=(mc == 0), stop=(mc == DC - 1))
            last.then_inc(g["fold_mm"], 1)
            pe.wait_ge(g["aw_rep"], START + 2)
            for mc in range(DC):
                last = nc.tensor.matmul(ps[:, 2, 0:D], BQR[:, mc, :], WQA[:, mc, :], start=(mc == 0), stop=(mc == DC - 1))
            last.then_inc(g["fold_mm"], 1)
            pe.wait_ge(g["aw_ready"], START + 4)

            def rows_to_columns(b, u, j):
                n = b * TPB + j
                pe.wait_ge(g["u_done"], START + n + 1)
                pe.wait_ge(g["gt_done"], START + n)
                for c in range(DC):
                    last = nc.tensor.transpose(ps[:, 2, c * P:(c + 1) * P], U[:, u, j, c * P:(c + 1) * P], ident)
                last.then_inc(g["gt_tr"], 1)

            def project(b, j):
                n = b * TPB + j
                pe.wait_ge(g["gt_done"], START + n + 1)
                pe.wait_ge(g["kv_done"], START + n)
                for i in range(2):
                    for c in range(DC):
                        last = nc.tensor.matmul(ps[:, i, :], GT[:, j, c, :], W[:, c, 2 * i:2 * i + 2, :].rearrange("p i n -> p (i n)"), start=(c == 0), stop=(c == DC - 1))
                last.then_inc(g["aproj_done"], 1)

            def first(b, u):
                rows_to_columns(b, u, 0)
                rows_to_columns(b, u, 1)
                project(b, 0)
                rows_to_columns(b, u, 2)
                project(b, 1)
                project(b, 2)

            def running_sum(bank, b, j, src, ready, used, count):
                n = b * TPB + j
                pe.wait_ge(g[ready], START + n + 1)
                pe.wait_ge(g[used], START + n)
                for i in range(j):
                    nc.tensor.matmul(ps[:, bank, 0:D], ones, src[:, i, :], start=(i == 0), stop=False)
                nc.tensor.matmul(ps[:, bank, 0:D], tri, src[:, j, :], start=(j == 0), stop=True).then_inc(g[count], 1)

            def mixed_transpose(b, j):
                n = b * TPB + j
                pe.wait_ge(g["m_done"], START + n + 1)
                pe.wait_ge(g["mt_done"], START + n)
                for c in range(DC):
                    last = nc.tensor.transpose(ps[:, 4, c * P:(c + 1) * P], Mx[:, j, c * P:(c + 1) * P], ident)
                last.then_inc(g["t2_tr"], 1)

            def key_logits(b, j):
                n = b * TPB + j
                pe.wait_ge(g["mt_done"], START + n + 1)
                pe.wait_ge(g["kl_done"], START + n)
                for c in range(DC):
                    last = nc.tensor.matmul(ps[:, 5, 0:D], MT[:, j, c, :], WKA[:, c, :], start=(c == 0), stop=(c == DC - 1))
                last.then_inc(g["klog_done"], 1)

            def body(b, u, fixed):
                if fixed is None or fixed < B - 1:
                    first(b + 1, 1 - u)

                def sum1(j):
                    running_sum(3, b, j, WQ, "wq_done", "m_done", "cum1_done")
                sum1(0)
                sum1(1)
                mixed_transpose(b, 0)
                sum1(2)
                mixed_transpose(b, 1)
                key_logits(b, 0)
                mixed_transpose(b, 2)
                key_logits(b, 1)
                key_logits(b, 2)
                for j in range(TPB):
                    running_sum(6, b, j, KW, "kw_done", "attn_out", "cum2_done")

            steps(pe, lambda: first(0, 0), body)

        @blk.scalar
        def _(act):
            act.wait_ge(g["wqT_tr"], START + 1)
            nc.scalar.activation(WQT[:].rearrange("p c n -> p (c n)"), ps[:, 0, :], ACT.Copy).then_inc(g["wqT_done"], 1)

            def first(b, u):
                for j in range(TPB):
                    n = b * TPB + j
                    act.wait_ge(g["gt_tr"], START + n + 1)
                    act.wait_ge(g["aproj_done"], START + n - 2)
                    for c in range(DC):
                        last = nc.scalar.activation(GT[:, j, c, :], ps[:, 2, c * P:(c + 1) * P], ACT.Identity, scale=COL[:, 0, c:c + 1], bias=COL[:, 1, c:c + 1])
                    last.then_inc(g["gt_done"], 1)

            def softmax(b, j, i, src, ready, count):
                act.wait_ge(g[ready], START + b * TPB + j + 1)
                nc.scalar.activation(src, src, ACT.Exp, bias=NM[:, i, j:j + 1], accum_out=SM[:, i, j:j + 1]).then_inc(g[count], 1)

            def body(b, u, fixed):
                for j in range(TPB):
                    softmax(b, j, 0, QA[:, u, j, 1, :], "max1_done", "exp1_done")
                if fixed is None or fixed < B - 1:
                    first(b + 1, 1 - u)
                for j in range(TPB):
                    n = b * TPB + j
                    act.wait_ge(g["t2_tr"], START + n + 1)
                    act.wait_ge(g["klog_done"], START + n - 2)
                    nc.scalar.activation(MT[:, j, :, :].rearrange("p c n -> p (c n)"), ps[:, 4, 0:D], ACT.Copy).then_inc(g["mt_done"], 1)
                for j in range(TPB):
                    softmax(b, j, 1, KL[:, j, :], "max2_done", "exp2_done")

            steps(act, lambda: first(0, 0), body)

        @blk.vector
        def _(dve):
            ch = Chain(dve, g["attn_chain"])
            dve.wait_ge(g["aw_load"], START + 16 * 13)
            for c in range(DC):
                nc.vector.tensor_scalar(out=BQR[:, c, :], in0=ones, scalar1=COL[:, 2, c:c + 1], scalar2=None, op0=ALU.mult).then_inc(g["aw_rep"], 1)
            dve.wait_ge(g["fold_mm"], START + 1)
            nc.vector.tensor_scalar(out=W[:, :, 1, :], in0=ps[:, 1, :].rearrange("p (c n) -> p c n", n=D), scalar1=SCALE, scalar2=None, op0=ALU.mult).then_inc(g["aw_ready"], 1)
            dve.wait_ge(g["fold_mm"], START + 2)
            ch.begin(0)
            ch.link(nc.vector.tensor_tensor(out=BI[:, 1, :], in0=ps[:, 2, 0:D], in1=BI[:, 1, :], op=ALU.add))
            nc.vector.tensor_scalar(out=BI[:, 1, :], in0=BI[:, 1, :], scalar1=SCALE, scalar2=None, op0=ALU.mult).then_inc(g["aw_ready"], 1)
            nc.vector.tensor_scalar(out=WKA[:], in0=WKA[:], scalar1=SCALE, scalar2=None, op0=ALU.mult).then_inc(g["aw_ready"], 1)
            nc.vector.tensor_scalar(out=BKA[:], in0=BKA[:], scalar1=SCALE, scalar2=None, op0=ALU.mult).then_inc(g["aw_ready"], 1)
            dve.wait_ge(g["aw_ready"], START + 4)
            PRE = 1

            def norm_rows(b, u):
                for j in range(TPB):
                    ch.link(nc.vector.bn_stats(ST[:, j, :], Hst(Hs, b * TPB + j)))
                    dve.sem_inc(g["attn_waited"], 1)
                    ch.link(nc.vector.bn_aggr(MV[:, j, :], ST[:, j, :]))
                nc.vector.tensor_scalar(out=VE[:], in0=MV[:, :, 1], scalar1=1.0 + EPS, scalar2=EPS * EPS, op0=ALU.mult, op1=ALU.add).then_inc(g["avar_done"], 1)
                dve.wait_ge(g["arstd_done"], START + b + 1)
                dve.wait_ge(g["gt_tr"], START + b * TPB - TPB)
                for j in range(TPB):
                    nc.vector.tensor_scalar(out=U[:, u, j, :], in0=Hst(Hs, b * TPB + j), scalar1=MV[:, j, 0:1], scalar2=RS[:, j:j + 1], op0=ALU.subtract, op1=ALU.mult).then_inc(g["u_done"], 1)

            def add_biases(b, u):
                for j in range(TPB):
                    dve.wait_ge(g["aproj_done"], START + b * TPB + j + 1)
                    nc.vector.tensor_tensor(out=QA[:, u, j, :, :].rearrange("p i n -> p (i n)"), in0=ps[:, 0, :], in1=BI[:, 0:2, :].rearrange("p i n -> p (i n)"), op=ALU.add)
                    nc.vector.tensor_tensor(out=KV[:, u, j, :, :].rearrange("p i n -> p (i n)"), in0=ps[:, 1, :], in1=BI[:, 2:4, :].rearrange("p i n -> p (i n)"), op=ALU.add).then_inc(g["kv_done"], 1)

            def weigh(b, j, i, e, x, to, ready, count):
                dve.wait_ge(g[ready], START + b * TPB + j + 1)
                ch.link(nc.vector.reciprocal(SM[:, i, j:j + 1], SM[:, i, j:j + 1]))
                nc.vector.scalar_tensor_tensor(out=to, in0=e, scalar=SM[:, i, j:j + 1], in1=x, op0=ALU.mult, op1=ALU.mult).then_inc(g[count], 1)

            def body(b, u, fixed):
                ch.begin(PRE + 4 * TPB + b * 5 * TPB - (2 * TPB if fixed == B - 1 else 0))
                for j in range(TPB):
                    dve.wait_ge(g["kv_done"], START + b * TPB + j + 1)
                    nc.vector.tensor_reduce(out=NM[:, 0, j:j + 1], in_=QA[:, u, j, 1, :], op=ALU.max, axis=AX.X, negate=True).then_inc(g["max1_done"], 1)
                for j in range(TPB):
                    weigh(b, j, 0, QA[:, u, j, 1, :], QA[:, u, j, 0, :], WQ[:, j, :], "exp1_done", "wq_done")
                if fixed is None or fixed < B - 1:
                    add_biases(b + 1, 1 - u)
                for j in range(TPB):
                    dve.wait_ge(g["cum1_done"], START + b * TPB + j + 1)
                    nc.vector.scalar_tensor_tensor(out=Mx[:, j, :], in0=ps[:, 3, 0:D], scalar=K[:, C_INV + j:C_INV + j + 1], in1=KV[:, u, j, 0, :], op0=ALU.mult, op1=ALU.mult).then_inc(g["m_done"], 1)
                for j in range(TPB):
                    n = b * TPB + j
                    dve.wait_ge(g["klog_done"], START + n + 1)
                    nc.vector.tensor_tensor(out=KL[:, j, :], in0=ps[:, 5, 0:D], in1=BKA[:], op=ALU.add).then_inc(g["kl_done"], 1)
                    dve.wait_ge(g["kl_done"], START + n + 1)
                    nc.vector.tensor_reduce(out=NM[:, 1, j:j + 1], in_=KL[:, j, :], op=ALU.max, axis=AX.X, negate=True).then_inc(g["max2_done"], 1)
                for j in range(TPB):
                    weigh(b, j, 1, KL[:, j, :], Mx[:, j, :], KW[:, j, :], "exp2_done", "kw_done")
                if fixed is None or fixed < B - 2:
                    norm_rows(b + 2, u)
                for j in range(TPB):
                    n = b * TPB + j
                    dve.wait_ge(g["cum2_done"], START + n + 1)
                    ch.link(nc.vector.scalar_tensor_tensor(out=TM[:, j, :], in0=ps[:, 6, 0:D], scalar=K[:, C_INV + j:C_INV + j + 1], in1=KV[:, u, j, 1, :], op0=ALU.mult, op1=ALU.mult))
                    nc.vector.tensor_tensor(out=Hst(Hs, n), in0=TM[:, j, :], in1=Hst(Hs, n), op=ALU.add).then_inc(g["attn_out"], 1)
                ch.end(5 * TPB if fixed is None or fixed < B - 2 else 3 * TPB)

            def before():
                norm_rows(0, 0)
                add_biases(0, 0)
                norm_rows(1, 1)

            ch.begin(PRE)
            steps(dve, before, body)


def router_phase(s, made):
    sem = s["sem"]
    if made is None:
        names = ["zeros_set", "xd_zeroed", "wg_load", "rvar_done", "rrstd_done", "r_rows", "r_tr", "rt_done", "r_kept", "logit_mm", "gap_done", "gap_exp", "picks_done",
                 "rank_mm", "slots_done", "sw_scattered", "router_chain", "router_waited"]
        return {n: sem(n) for n in names}
    g = made
    nc, a, K, ident, Hs, ps, sb = s["nc"], s["a"], s["K"], s["ident"], s["Hs"], s["ps"], s["sb"]
    SI, GI, WT = s["scatter_at"], s["gather_at"], s["mix_weights"]
    R = 4
    NS = TOPK * NT
    Z0 = sb("zeros", [P, 15, D])
    WG = sb("w_gate", [P, DC, E])
    X3 = sb("x_norm", [P, NT, D])
    U = sb("r_rows_ring", [P, R, D])
    UT = sb("r_rowsT", [P, R, DC, P])
    ST = sb("r_st", [P, NT, 6])
    MV = sb("r_mv", [P, NT, 2])
    VE = sb("r_ve", [P, NT])
    RS = sb("r_rs", [P, NT])
    LG = sb("logits", [P, NT, E])
    REV = sb("reversed_index", [P, E])
    TP = sb("top", [P, TOPK, NT])
    EQ = sb("r_eq", [P, NT, E])
    IX = sb("r_ix", [P, NT])
    OH = sb("onehot", [P, TOPK, NT, E])
    GAP = sb("gap", [P, NT])
    TOT = sb("totals", [P, NS, E])
    INC = sb("running", [P, NS, E])
    ZZ = sb("zero_row", [P, NS])
    KO = sb("kept_onehot", [P, NS, E])
    KEPT = sb("kept", [P, NS])
    SL = sb("slots", [P, NS])
    SC = sb("slots_scatter", [P, NS])

    blk = nc.Block()
    with blk:
        @blk.sync
        def _(sp):
            sp.dma_start(WG[:], a["L0_ffn_w_g"].rearrange("(c p) e -> p c e", p=P)).then_inc(g["wg_load"], 16)
            sp.wait_ge(g["zeros_set"], START + 1)
            for i in range(4):
                sp.dma_start(s["xd"][i * 15 * P:(i + 1) * 15 * P, :].rearrange("(p r) d -> p r d", p=P), Z0[:]).then_inc(g["xd_zeroed"], 16)

        @blk.gpsimd
        def _(pool):
            pool.memset(Z0[:], 0.0).then_inc(g["zeros_set"], 1)
            pool.wait_ge(g["rvar_done"], START + 1)
            nc.gpsimd.tensor_tensor(out=RS[:], in0=VE[:], in1=K[:, C_NHALF:C_NHALF + 1].to_broadcast([P, NT]), op=ALU.pow).then_inc(g["rrstd_done"], 1)
            pool.wait_ge(g["xd_zeroed"], START + 64)
            pool.wait_ge(g["r_kept"], START + NT)
            pool.wait_ge(g["slots_done"], START + 1)
            for k in range(TOPK):
                for i in range(NT):
                    pool.indirect_dma_start(out=s["xd"], out_offset=bass.IndirectOffsetOnAxis(ap=SI[:, k * NT + i:k * NT + i + 1], axis=0),
                                            in_=X3[:, i, :], in_offset=None).then_inc(g["sw_scattered"], 16)
            pool.wait_ge(g["sw_scattered"], 16 * NS)

        @blk.tensor
        def _(pe):
            pe.wait_ge(g["wg_load"], START + 16)
            with pe.Fori(0, NT // R) as q:
                for r in range(R):
                    n = q * R + r
                    pe.wait_ge(g["r_rows"], START + n + 1)
                    pe.wait_ge(g["rt_done"], START + n - 1)
                    for c in range(DC):
                        last = nc.tensor.transpose(ps[:, r % 2, c * P:(c + 1) * P], U[:, r, c * P:(c + 1) * P], ident)
                    last.then_inc(g["r_tr"], 1)
                for r in range(R):
                    n = q * R + r
                    pe.wait_ge(g["rt_done"], START + n + 1)
                    for c in range(DC):
                        last = nc.tensor.matmul(ps[:, 2, bass.ds(n * E, E)], UT[:, r, c, :], WG[:, c, :], start=(c == 0), stop=(c == DC - 1))
                    last.then_inc(g["logit_mm"], 1)
            pe.wait_ge(g["picks_done"], START + 1)
            oh = OH[:].rearrange("p k t e -> p (k t e)")
            nc.tensor.matmul(ps[:, 3, 0:NS * E], s["stri"], oh, start=True, stop=True)
            nc.tensor.matmul(ps[:, 4, 0:NS * E], s["ones"], oh, start=True, stop=True).then_inc(g["rank_mm"], 1)

        @blk.scalar
        def _(act):
            with act.Fori(0, NT // R) as q:
                for r in range(R):
                    n = q * R + r
                    act.wait_ge(g["r_tr"], START + n + 1)
                    act.wait_ge(g["logit_mm"], START + n - 3)
                    nc.scalar.activation(UT[:, r, :, :].rearrange("p c n -> p (c n)"), ps[:, r % 2, 0:D], ACT.Copy).then_inc(g["rt_done"], 1)
                    nc.scalar.activation(Hst(X3, n), U[:, r, :], ACT.Copy).then_inc(g["r_kept"], 1)
            act.wait_ge(g["gap_done"], START + 1)
            nc.scalar.activation(GAP[:], GAP[:], ACT.Exp).then_inc(g["gap_exp"], 1)

        @blk.vector
        def _(dve):
            ch = Chain(dve, g["router_chain"])
            ch.begin(0)
            with dve.Fori(0, NT) as n:
                ch.begin(n)
                ch.link(nc.vector.bn_stats(ST[:, bass.ds(n, 1), :].rearrange("p o s -> p (o s)"), Hst(Hs, n)))
                ch.end(1)
            ch.begin(NT)
            for n in range(NT):
                last = nc.vector.bn_aggr(MV[:, n, :], ST[:, n, :])
            ch.link(last)
            nc.vector.tensor_scalar(out=VE[:], in0=MV[:, :, 1], scalar1=EPS, scalar2=None, op0=ALU.add).then_inc(g["rvar_done"], 1)
            dve.wait_ge(g["rrstd_done"], START + 1)
            with dve.Fori(0, NT // R) as q:
                for r in range(R):
                    n = q * R + r
                    dve.wait_ge(g["r_kept"], START + n - 3)
                    dve.wait_ge(g["r_tr"], START + n - 3)
                    nc.vector.tensor_scalar(out=U[:, r, :], in0=Hst(Hs, n), scalar1=MV[:, bass.ds(n, 1), 0:1].rearrange("p o s -> p (o s)"),
                                            scalar2=RS[:, bass.ds(n, 1)], op0=ALU.subtract, op1=ALU.mult).then_inc(g["r_rows"], 1)
            dve.wait_ge(g["logit_mm"], START + NT)
            ch.link(nc.vector.tensor_copy(LG[:].rearrange("p t e -> p (t e)"), ps[:, 2, 0:NT * E]))
            ch.link(nc.vector.tensor_scalar(out=REV[:], in0=K[:, C_IOTA:C_IOTA + E], scalar1=-1.0, scalar2=float(E), op0=ALU.mult, op1=ALU.add))
            ch.link(nc.vector.memset(ZZ[:], 0.0))
            rev = REV[:, None, :].to_broadcast([P, NT, E])
            for k in range(TOPK):
                ch.link(nc.vector.tensor_reduce(out=TP[:, k, :], in_=LG[:], op=ALU.max, axis=AX.X))
                ch.link(nc.vector.tensor_tensor(out=EQ[:], in0=LG[:], in1=TP[:, k, :, None].to_broadcast([P, NT, E]), op=ALU.is_equal))
                ch.link(nc.vector.tensor_tensor(out=EQ[:], in0=EQ[:], in1=rev, op=ALU.mult))
                ch.link(nc.vector.tensor_reduce(out=IX[:], in_=EQ[:], op=ALU.max, axis=AX.X))
                ch.link(nc.vector.tensor_tensor(out=OH[:, k, :, :], in0=rev, in1=IX[:, :, None].to_broadcast([P, NT, E]), op=ALU.is_equal))
                if k == 0:
                    ch.link(nc.vector.tensor_scalar(out=EQ[:], in0=OH[:, 0, :, :], scalar1=-1.0, scalar2=1.0, op0=ALU.mult, op1=ALU.add))
                    ch.link(nc.vector.tensor_tensor(out=LG[:], in0=LG[:], in1=EQ[:], op=ALU.mult))
                    ch.link(nc.vector.tensor_scalar(out=EQ[:], in0=OH[:, 0, :, :], scalar1=-3e38, scalar2=None, op0=ALU.mult))
                    ch.link(nc.vector.tensor_tensor(out=LG[:], in0=LG[:], in1=EQ[:], op=ALU.add))
            nc.vector.sem_inc(g["picks_done"], 1)
            nc.vector.tensor_tensor(out=GAP[:], in0=TP[:, 1, :], in1=TP[:, 0, :], op=ALU.subtract).then_inc(g["gap_done"], 1)
            dve.wait_ge(g["rank_mm"], START + 1)
            ch.link(nc.vector.tensor_copy(TOT[:].rearrange("p s e -> p (s e)"), ps[:, 4, 0:NS * E]))
            for e in range(E):
                last = nc.vector.tensor_tensor_scan(out=INC[:, :, e], data0=TOT[:, :, e], data1=ZZ[:], initial=0.0, op0=ALU.add, op1=ALU.add)
            ch.link(last)
            ch.link(nc.vector.tensor_tensor(out=INC[:], in0=INC[:], in1=TOT[:], op=ALU.subtract))
            ch.link(nc.vector.tensor_tensor(out=INC[:].rearrange("p s e -> p (s e)"), in0=ps[:, 3, 0:NS * E], in1=INC[:].rearrange("p s e -> p (s e)"), op=ALU.add))
            oh = OH[:].rearrange("p k t e -> p (k t) e")
            ch.link(nc.vector.scalar_tensor_tensor(out=KO[:].rearrange("p s e -> p (s e)"), in0=INC[:].rearrange("p s e -> p (s e)"), scalar=float(CAP), in1=OH[:].rearrange("p k t e -> p (k t e)"), op0=ALU.is_lt, op1=ALU.mult))
            ch.link(nc.vector.tensor_reduce(out=KEPT[:], in_=KO[:], op=ALU.add, axis=AX.X))
            ch.link(nc.vector.tensor_tensor(out=INC[:], in0=INC[:], in1=K[:, None, C_E960:C_E960 + E].to_broadcast([P, NS, E]), op=ALU.add))
            ch.link(nc.vector.tensor_tensor(out=INC[:], in0=INC[:], in1=KO[:], op=ALU.mult))
            ch.link(nc.vector.tensor_reduce(out=SL[:], in_=INC[:], op=ALU.add, axis=AX.X))
            ch.link(nc.vector.tensor_scalar(out=SC[:], in0=KEPT[:], scalar1=-1.0, scalar2=1.0, op0=ALU.mult, op1=ALU.add))
            ch.link(nc.vector.tensor_tensor(out=SC[:], in0=SC[:], in1=K[:, C_TRASH:C_PE], op=ALU.mult))
            ch.link(nc.vector.tensor_tensor(out=SC[:], in0=SC[:], in1=SL[:], op=ALU.add))
            ch.link(nc.vector.tensor_copy(GI[:], SL[:]))
            nc.vector.tensor_copy(SI[:], SC[:]).then_inc(g["slots_done"], 1)
            dve.wait_ge(g["gap_exp"], START + 1)
            ch.link(nc.vector.tensor_scalar(out=IX[:], in0=GAP[:], scalar1=1.0, scalar2=None, op0=ALU.add))
            ch.link(nc.vector.reciprocal(WT[:, 0, :], IX[:]))
            ch.link(nc.vector.tensor_tensor(out=WT[:, 1, :], in0=WT[:, 0, :], in1=GAP[:], op=ALU.mult))
            ch.link(nc.vector.tensor_tensor(out=WT[:].rearrange("p k t -> p (k t)"), in0=WT[:].rearrange("p k t -> p (k t)"), in1=KEPT[:], op=ALU.mult))


def expert_phase(s, made):
    sem = s["sem"]
    if made is None:
        names = ["ew_loaded0", "ew_loaded1", "xe_loaded0", "xe_loaded1", "xe_tr", "xt_act", "xt_dve", "fc_mm", "gelu_done", "down_mm", "ye_done", "y_stored0", "y_stored1",
                 "sw_gather0", "sw_gather1", "sw_gather2", "sw_gather3", "mix1_done", "mixed", "out_stored"]
        return {n: sem(n) for n in names}
    g = made
    nc, a, K, ident, Hs, ps, sb = s["nc"], s["a"], s["K"], s["ident"], s["Hs"], s["ps"], s["sb"]
    GI, WT = s["gather_at"], s["mix_weights"]
    TH = CTN // 2
    FC = [sb(f"w_fc{i}", [P, DC, M]) for i in range(2)]
    PJ = [sb(f"w_proj{i}", [P, MC, D]) for i in range(2)]
    XE = sb("x_expert", [CT, 2, TH, D])
    XT = sb("x_expertT", [P, 2, DC, HALF])
    GH = sb("gelu_out", [P, 2, MC, HALF])
    YO = sb("y_rows", [CT, 2, TH, D])
    R = 4
    GA = sb("gathered", [P, R, TOPK, D])
    xd = s["xd"][0:SLOTS, :].rearrange("(s t p) d -> s p t d", t=TH, p=CT)
    yd = s["yd"].rearrange("(s t p) d -> s p t d", t=TH, p=CT)
    FCB = (2, 3, 4, 7)
    STEPS = 2 * E

    def steps(eng, body):
        with eng.Fori(0, STEPS // 4 - 1) as q:
            for i in range(4):
                body(q * 4 + i, i, q, i + 0)
        for i in range(4):
            body(STEPS - 4 + i, i, STEPS // 4 - 1, STEPS - 4 + i)

    blk = nc.Block()
    with blk:
        @blk.sync
        def _(sp):
            def step(n, i, q):
                h, e = i % 2, q * 2 + i // 2
                if h == 0:
                    done = g[f"ew_loaded{i // 2}"]
                    sp.wait_ge(g["down_mm"], START + e * CTN - CTN)
                    sp.dma_start(FC[i // 2][:], a["L0_ffn_c_fc"][bass.ds(e, 1)].rearrange("o (c p) n -> p (o c) n", p=P)).then_inc(done, 16)
                    sp.dma_start(PJ[i // 2][:], a["L0_ffn_c_proj"][bass.ds(e, 1)].rearrange("o (c p) n -> p (o c) n", p=P)).then_inc(done, 16)
                sp.wait_ge(g["xe_tr"], START + 2 * n - 2)
                sp.dma_start(XE[:, h, :, :], xd[bass.ds(n, 1)].rearrange("o p t d -> p (o t) d")).then_inc(g[f"xe_loaded{h}"], 16)
                if not (isinstance(n, int) and n < 2):
                    store(n - 2, h)

            def store(n, h):
                sp.wait_ge(g["ye_done"], START + n * TH + TH)
                sp.dma_start(yd[bass.ds(n, 1)].rearrange("o p t d -> p (o t) d"), YO[:, h, :, :]).then_inc(g[f"y_stored{h}"], 16)

            for i in range(4):
                step(i, i, 0)
            with sp.Fori(1, STEPS // 4) as q:
                for i in range(4):
                    step(q * 4 + i, i, q)
            store(STEPS - 2, 0)
            store(STEPS - 1, 1)
            for i in range(NT):
                sp.wait_ge(g["mixed"], START + i + 1)
                sp.dma_start(s["out"][i // TPB, (i % TPB) * P:(i % TPB + 1) * P, :], Hs[:, i, :]).then_inc(g["out_stored"], 16)
            sp.wait_ge(g["out_stored"], START + 16 * NT)

        @blk.gpsimd
        def _(pool):
            pool.wait_ge(g["y_stored0"], START + 16 * E)
            pool.wait_ge(g["y_stored1"], START + 16 * E)
            for i in range(NT):
                if i >= R:
                    pool.wait_ge(g["mixed"], START + i - R + 1)
                for k in range(TOPK):
                    pool.indirect_dma_start(out=GA[:, i % R, k, :], out_offset=None, in_=s["yd"],
                                            in_offset=bass.IndirectOffsetOnAxis(ap=GI[:, k * NT + i:k * NT + i + 1], axis=0)).then_inc(g[f"sw_gather{i % R}"], 16)

        @blk.tensor
        def _(pe):
            def columns(n, h, lp):
                pe.wait_ge(g[f"xe_loaded{h}"], START + 16 * lp + 16)
                for c in range(DC):
                    pe.wait_ge(g["xt_act" if c == 0 else "xt_dve"], START + n)
                    for t in range(TH):
                        last = nc.tensor.transpose(ps[:, c, t * CT:(t + 1) * CT], XE[:, h, t, c * P:(c + 1) * P], ident[0:CT, 0:CT])
                    last.then_inc(g["xe_tr"], 1)

            def up(n, h, slot, wl):
                pe.wait_ge(g[f"ew_loaded{slot}"], START + 32 * wl + 32)
                pe.wait_ge(g["xt_act"], START + n + 1)
                pe.wait_ge(g["xt_dve"], START + n + 1)
                for m in range(MC):
                    pe.wait_ge(g["gelu_done"], START + n * MC + (m - 3))
                    for c in range(DC):
                        last = nc.tensor.matmul(ps[:, FCB[m % 4], 0:HALF], FC[slot][:, c, m * P:(m + 1) * P], XT[:, h, c, :], start=(c == 0), stop=(c == DC - 1))
                    last.then_inc(g["fc_mm"], 1)

            def down(n, h, slot):
                for t in range(TH):
                    pe.wait_ge(g["gelu_done"], START + n * MC + MC)
                    pe.wait_ge(g["ye_done"], START + n * TH + (t - 1))
                    for m in range(MC):
                        last = nc.tensor.matmul(ps[0:CT, 5 + t % 2, 0:D], GH[:, h, m, t * CT:(t + 1) * CT], PJ[slot][:, m, :], start=(m == 0), stop=(m == MC - 1))
                    last.then_inc(g["down_mm"], 1)

            def body(n, i, q, known):
                if not (isinstance(n, int) and n + 1 >= STEPS):
                    up(n + 1, (i + 1) % 2, ((i + 1) // 2) % 2, q + (i + 1) // 4)
                if not (isinstance(n, int) and n + 2 >= STEPS):
                    columns(n + 2, i % 2, q * 2 + (i + 2) // 2)
                down(n, i % 2, i // 2)

            columns(0, 0, 0)
            up(0, 0, 0, 0)
            columns(1, 1, 0)
            steps(pe, body)

        @blk.scalar
        def _(act):
            def body(n, i, q, known):
                h = i % 2
                act.wait_ge(g["fc_mm"], START + n * MC - MC)
                act.wait_ge(g["xe_tr"], START + 2 * n + 1)
                nc.scalar.activation(XT[:, h, 0, :], ps[:, 0, 0:HALF], ACT.Copy).then_inc(g["xt_act"], 1)
                act.wait_ge(g["down_mm"], START + n * TH - TH)
                for m in range(MC):
                    act.wait_ge(g["fc_mm"], START + n * MC + m + 1)
                    nc.scalar.activation(GH[:, h, m, :], ps[:, FCB[m % 4], 0:HALF], ACT.Gelu).then_inc(g["gelu_done"], 1)
            steps(act, body)

        @blk.vector
        def _(dve):
            def rows_out(n, h, st):
                dve.wait_ge(g[f"y_stored{h}"], START + 16 * st)
                for t in range(TH):
                    dve.wait_ge(g["down_mm"], START + n * TH + t + 1)
                    nc.vector.tensor_copy(YO[:, h, t, :], ps[0:CT, 5 + t % 2, 0:D]).then_inc(g["ye_done"], 1)

            def columns_out(n, h):
                dve.wait_ge(g["fc_mm"], START + n * MC - MC)
                dve.wait_ge(g["xe_tr"], START + 2 * n + 2)
                nc.vector.tensor_copy(XT[:, h, 1, :], ps[:, 1, 0:HALF]).then_inc(g["xt_dve"], 1)

            def body(n, i, q, known):
                if not (isinstance(n, int) and n + 2 >= STEPS):
                    columns_out(n + 2, i % 2)
                rows_out(n, i % 2, q * 2 + i // 2)

            columns_out(0, 0)
            columns_out(1, 1)
            steps(dve, body)
            for i in range(NT):
                dve.wait_ge(g[f"sw_gather{i % R}"], 32 * (i // R + 1))
                nc.vector.scalar_tensor_tensor(out=Hs[:, i, :], in0=GA[:, i % R, 0, :], scalar=WT[:, 0, i:i + 1], in1=Hs[:, i, :], op0=ALU.mult, op1=ALU.add).then_inc(g["mix1_done"], 1)
                dve.wait_ge(g["mix1_done"], START + i + 1)
                nc.vector.scalar_tensor_tensor(out=Hs[:, i, :], in0=GA[:, i % R, 1, :], scalar=WT[:, 1, i:i + 1], in1=Hs[:, i, :], op0=ALU.mult, op1=ALU.add).then_inc(g["mixed"], 1)




def _constants():
    import numpy as np
    k = np.zeros((P, C_ALL), np.float32)
    i = np.arange(P)
    k[:, C_ID:C_ID + P] = np.eye(P)
    k[:, C_TRI:C_TRI + P] = i[:, None] <= i[None, :]
    k[:, C_STRI:C_STRI + P] = i[:, None] < i[None, :]
    k[:, C_ONE:C_ONE + P] = 1.0
    k[:, C_EO] = (i % 32) < 16
    k[:, C_EO + 1] = (i % 32) >= 16
    for t in range(TPB):
        k[:, C_INV + t] = np.float32(1.0) / (t * P + i + 1).astype(np.float32)
    k[:, C_IOTA:C_IOTA + E] = np.arange(E)
    k[:, C_E960:C_E960 + E] = np.arange(E) * CAP
    k[:, C_TRASH:C_PE] = SLOTS + P * np.arange(TOPK * NT)[None, :] + i[:, None]
    k[:, C_NHALF] = -0.5
    pos = np.arange(L_TXT, dtype=np.float32)[:, None]
    div = np.exp(np.arange(0, D, 2, dtype=np.float32) * np.float32(-np.log(np.float32(10000.0)) / np.float32(D)))
    ang = (pos * div).astype(np.float32)
    k[:, C_PE:C_PE + D:2] = np.sin(ang)
    k[:, C_PE + 1:C_PE + D:2] = np.cos(ang)
    return k


def kernel(**inputs):
    import numpy as _np
    import concourse.bacc as _bacc
    from concourse import mybir as _mybir
    from concourse.bass_utils import run_bass_kernel_spmd as _run
    nc = _bacc.Bacc("TRN2", target_bir_lowering=False, num_devices=1)
    arrays, a = {}, {}
    inputs = dict(inputs)
    inputs["const"] = _constants()
    for name, v in inputs.items():
        v = _np.ascontiguousarray(v)
        if v.dtype == _np.bool_:
            v = v.view(_np.int32)
        arrays[f"in_{name}"] = v
        a[name] = nc.dram_tensor(f"in_{name}", v.shape, _mybir.dt.from_np(v.dtype), kind="ExternalInput").ap()
    out = nc.dram_tensor("out", (B, TPB * P, D), F32, kind="ExternalOutput").ap()
    program(nc, a, out)
    r = _run(nc, [arrays], core_ids=[0])
    return r.results[0]["out"]
```

```python
import concourse.bass as bass
from concourse import mybir
from contextlib import ExitStack

F32 = mybir.dt.float32
I32 = mybir.dt.int32
U32 = mybir.dt.uint32
U8 = mybir.dt.uint8
BF16 = mybir.dt.bfloat16
F32R = mybir.dt.float32r
ACT = mybir.ActivationFunctionType
ALU = mybir.AluOpType
AX = mybir.AxisListType

P = 128
B, F, L_TOK, HT = 8, 64, 256, 4
D = 256
DC = D // P
L_TXT = 128
VOCAB, H, KD, M, LAYERS = 8000, 16, 16, 1024, 4
MC = M // P
TPB = (L_TOK + L_TXT) // P
NT = B * TPB
E, TOPK = 8, 2
N = NT * P
CAP = int(TOPK * 1.25 * N / E)
CAP += CAP % 2
SLOTS = E * CAP
CT = 120
CTN = CAP // CT
HALF = CAP // 2
EPS = 1e-5
START = 64

C_ID, C_TRI, C_STRI, C_ONE = 0, 128, 256, 384
C_EO, C_INV, C_IOTA, C_E960, C_NHALF = 512, 514, 517, 525, 533
C_TRASH = 534
C_PE = C_TRASH + TOPK * NT
C_ALL = C_PE + D


class Chain:

    def __init__(self, eng, sem):
        self.eng, self.sem, self.base, self.n = eng, sem, START, 0

    def begin(self, done):
        self.base, self.n = START + done, 0

    def link(self, ins):
        self.n += 1
        ins.then_inc(self.sem, 1)
        self.eng.wait_ge(self.sem, self.base + self.n)

    def end(self, per):
        assert self.n == per, self.n


def program(nc, a, out):
    with ExitStack() as ctx:
        def sb(name, shape, dt=F32):
            return ctx.enter_context(nc.sbuf_tensor(name, shape, dt))

        sems = []

        def sem(name):
            s = ctx.enter_context(nc.semaphore(name))
            if not name.startswith("sw_"):
                sems.append(s)
            return s

        K = sb("consts", [P, C_ALL])
        ident = K[:, C_ID:C_ID + P]
        tri = K[:, C_TRI:C_TRI + P]
        stri = K[:, C_STRI:C_STRI + P]
        ones = K[:, C_ONE:C_ONE + P]
        Hs = sb("hidden", [P, NT, D])
        ps = ctx.enter_context(nc.psum_tensor("banks", [P, 8, 512], F32))
        s = dict(nc=nc, a=a, out=out, sem=sem, K=K, ident=ident, tri=tri, stri=stri, ones=ones, Hs=Hs, ps=ps)
        phases = [tok_phase, txt_phase, attn_phase, router_phase, expert_phase]
        s["xd"] = nc.dram_tensor("dispatched", [SLOTS + TOPK * N, D], F32, kind="Internal").ap()
        s["yd"] = nc.dram_tensor("expert_out", [SLOTS, D], F32, kind="Internal").ap()
        s["out_stats"] = sb("out_stats", [P, NT, 6])
        s["scatter_at"] = sb("scatter_at", [P, TOPK * NT], I32)
        s["gather_at"] = sb("gather_at", [P, TOPK * NT], I32)
        s["mix_weights"] = sb("mix_weights", [P, TOPK, NT])
        k_ld = ctx.enter_context(nc.semaphore("consts_loaded"))
        built = []
        for f in phases:
            built.append((f, f(s, None)))
        blk = nc.Block()
        with blk:
            @blk.sync
            def _(sp):
                sp.dma_start(K[:], a["const"]).then_inc(k_ld, 16)
                sp.wait_ge(k_ld, 16)
                for x in sems:
                    sp.sem_inc(x, START)
        for f, made in built:
            s[f.__name__] = made
        attn_mem, txt_mem, expert_mem = ExitStack(), ExitStack(), ExitStack()

        def shared(mem, *shape):
            return mem.enter_context(nc.sbuf_tensor(*shape))
        s["attn_w"] = dict(W=shared(attn_mem, "a_w", [P, DC, 4, D], F32), WKA=shared(attn_mem, "a_wka", [P, DC, D], F32), WQA=shared(attn_mem, "a_wqa", [P, DC, D], F32),
                           BI=shared(attn_mem, "a_bias", [P, 4, D], F32), BKA=shared(attn_mem, "a_bka", [P, D], F32), COL=shared(attn_mem, "a_cols", [P, 3, DC], F32))
        s["txt_w"] = [dict(qkv=shared(txt_mem, f"w_qkv{p}", [P, DC, 3, D], F32), wc=shared(txt_mem, f"w_c{p}", [P, DC, D], F32), w1=shared(txt_mem, f"w_1{p}", [P, DC, M], F32),
                           w2=shared(txt_mem, f"w_2{p}", [P, MC, D], F32), vec=shared(txt_mem, f"w_vec{p}", [P, 5, D], F32), b1=shared(txt_mem, f"w_b1{p}", [P, MC], F32)) for p in range(2)]
        s["ids"] = [shared(txt_mem, n, [P, B], t) for n, t in (("ids", I32), ("ids_f", F32), ("ids_neg", F32))]
        for f, made in built:
            if f is attn_phase:
                txt_mem.close()
            if f is router_phase:
                attn_mem.close()
                s["expert_w"] = dict(WS=shared(expert_mem, "w_raw", [P, 2, DC * M], F32),
                                     FC=[shared(expert_mem, f"w_fc_{x}0", [P, DC, M], F32R) for x in ("hi", "lo")],
                                     PJ=[shared(expert_mem, f"w_proj_{x}0", [P, MC, D], F32R) for x in ("hi", "lo")])
            with ExitStack() as mem:
                def sbp(name, shape, dt=F32):
                    return mem.enter_context(nc.sbuf_tensor(name, shape, dt))
                s["sb"] = sbp
                f(s, made)
        expert_mem.close()


def Hst(Hs, tile, c=None):
    x = Hs[:, bass.ds(tile, 1), :].rearrange("p o d -> p (o d)")
    return x if c is None else x[:, c * P:(c + 1) * P]


def load_text_layer(sp, s, lay, p):
    a, w, done = s["a"], s["txt_w"][p], s["txt_phase"][f"w_loaded{p}"]

    def at(n):
        return a["L0_txt_" + n]
    for i, n in enumerate(("Wq", "Wk", "Wv")):
        sp.dma_start(w["qkv"][:, :, i, :], at(n)[bass.ds(lay, 1)].rearrange("o (c p) n -> p (o c) n", p=P)).then_inc(done, 16)
    sp.dma_start(w["wc"][:], at("Wc")[bass.ds(lay, 1)].rearrange("o (c p) n -> p (o c) n", p=P)).then_inc(done, 16)
    sp.dma_start(w["w1"][:], at("W1")[bass.ds(lay, 1)].rearrange("o (c p) n -> p (o c) n", p=P)).then_inc(done, 16)
    sp.dma_start(w["w2"][:], at("W2")[bass.ds(lay, 1)].rearrange("o (c p) n -> p (o c) n", p=P)).then_inc(done, 16)
    for i, n in enumerate(("b2", "g1", "be1", "g2", "be2")):
        sp.dma_start(w["vec"][:, i, :], at(n)[bass.ds(lay, 1), :].to_broadcast([P, D])).then_inc(done, 16)
    sp.dma_start(w["b1"][:], at("b1")[bass.ds(lay, 1), :].rearrange("o (c p) -> p (o c)", p=P), allow_slow_non_contiguous=True).then_inc(done, 16)


def load_attn(sp, s):
    a, done, w = s["a"], s["attn_phase"]["aw_load"], s["attn_w"]
    for i, n in ((0, "Wq"), (2, "Wk"), (3, "Wv")):
        sp.dma_start(w["W"][:, :, i, :], a["L0_attn_" + n].rearrange("(c p) n -> p c n", p=P)).then_inc(done, 16)
    sp.dma_start(w["WQA"][:], a["L0_attn_Wqa"].rearrange("(c p) n -> p c n", p=P)).then_inc(done, 16)
    sp.dma_start(w["WKA"][:], a["L0_attn_Wka"].rearrange("(c p) n -> p c n", p=P)).then_inc(done, 16)
    for i, n in enumerate(("bq", "bqa", "bk", "bv")):
        sp.dma_start(w["BI"][:, i, :], a["L0_attn_" + n].partition_broadcast(P)).then_inc(done, 16)
    sp.dma_start(w["BKA"][:], a["L0_attn_bka"].partition_broadcast(P)).then_inc(done, 16)
    for i, n in enumerate(("gamma", "beta", "bq")):
        sp.dma_start(w["COL"][:, i, :], a["L0_attn_" + n].rearrange("(c p) -> p c", p=P), allow_slow_non_contiguous=True).then_inc(done, 16)


def load_expert(sp, s, e):
    a, g, WS = s["a"], s["expert_phase"], s["expert_w"]["WS"]
    sp.dma_start(WS[:, 0, :].rearrange("p (c n) -> p c n", c=DC), a["L0_ffn_c_fc"][bass.ds(e, 1)].rearrange("o (c p) n -> p (o c) n", p=P)).then_inc(g["ew_loaded0"], 16)
    sp.dma_start(WS[:, 1, :].rearrange("p (c n) -> p c n", c=MC), a["L0_ffn_c_proj"][bass.ds(e, 1)].rearrange("o (c p) n -> p (o c) n", p=P)).then_inc(g["ew_loaded1"], 16)


def tok_phase(s, made):
    sem = s["sem"]
    if made is None:
        names = ["tw_load", "tw_mask", "tw_exp", "tw_tr", "tw_ready", "x_loaded0", "x_loaded1", "proj_done", "tokact_done", "ekv_done",
                 "mix_done", "y_done", "yt_tr", "yt_done", "o_done", "tvar_done", "trstd_done", "tok_out",
                 "tok_chain", "waited", "tz_scaled"]
        return {n: sem(n) for n in names}
    g = made
    nc, a, K, ident, Hs, ps, sb = s["nc"], s["a"], s["K"], s["ident"], s["Hs"], s["ps"], s["sb"]
    wraw = sb("tok_wraw", [F, 3, F])
    WT = sb("tok_wt", [F + 1, HT, 4 * F])
    wb = sb("tok_wbias", [P, 2, L_TOK])
    msk = sb("tok_mask", [P, 2, L_TOK // 4], I32)
    ewT = sb("tok_ewT", [P, 2, L_TOK])
    ow = sb("tok_outw", [P, DC, D])
    gb = sb("tok_gb", [P, 2, D])
    X1 = sb("tok_x", [F + 1, 2, L_TOK * HT])
    EK = sb("tok_ek", [P, 2, 2, 2 * D])
    EQ = sb("tok_eq", [P, 2, 2, D])
    XR = sb("tok_xr", [P, 2, 2, D])
    DEN = sb("tok_den", [P, 2, D])
    Y = sb("tok_y", [P, 2, D])
    YT = sb("tok_yT", [P, 2, DC, P])
    Z = sb("tok_z", [P, 2, D])
    ST = sb("tok_st", [P, 2, 6])
    MV = sb("tok_mv", [P, 2, 2])
    VE = sb("tok_ve", [P, 2])
    RS = sb("tok_rs", [P, 2])
    x = a["x"].rearrange("n c l h -> n c (l h)")
    ids, idf, idn = s["ids"]
    txt = s["txt_phase"]

    blk = nc.Block()
    with blk:
        @blk.sync
        def _(sp):
            sp.dma_start(ids[:], a["x_txt"].rearrange("b n -> n b"), allow_slow_non_contiguous=True).then_inc(txt["ids_loaded"], 16)
            for i, n in enumerate(("L0_tok_Wq_w", "L0_tok_Wk_w", "L0_tok_Wv_w")):
                sp.dma_start(wraw[:, i, :], a[n]).then_inc(g["tw_load"], 16)
            sp.dma_start(wb[:], a["L0_tok_w_bias"].rearrange("(c p) s -> p c s", p=P)).then_inc(g["tw_load"], 16)
            sp.dma_start(msk[:], a["L0_tok_local_mask"].rearrange("(c p) s -> p c s", p=P)).then_inc(g["tw_load"], 16)
            sp.dma_start(ow[:], a["L0_tok_out_w"].rearrange("(c p) n -> p c n", p=P)).then_inc(g["tw_load"], 16)
            sp.dma_start(gb[:, 0, :], a["L0_tok_ln_g"].partition_broadcast(P)).then_inc(g["tw_load"], 16)
            sp.dma_start(gb[:, 1, :], a["L0_tok_ln_b"].partition_broadcast(P)).then_inc(g["tw_load"], 16)
            for h in range(HT):
                for i, n in enumerate(("L0_tok_Wq_b", "L0_tok_Wk_b", "L0_tok_Wv_b")):
                    sp.dma_start(WT[F:F + 1, h, i * F:(i + 1) * F], a[n].rearrange("(o n) -> o n", o=1)).then_inc(g["tw_load"], 16)
                sp.dma_start(WT[F:F + 1, h, 3 * F:], a["L0_tok_out_b"][h * F:(h + 1) * F].rearrange("(o n) -> o n", o=1)).then_inc(g["tw_load"], 16)
            with sp.Fori(0, B // 2) as tp:
                for u in range(2):
                    t = tp * 2 + u
                    sp.wait_ge(g["proj_done"], START + 2 * t - 2)
                    sp.dma_start(X1[0:F, u, :], x[bass.ds(t, 1), :, :].rearrange("o c n -> (o c) n")).then_inc(g[f"x_loaded{u}"], 16)
            for p in range(2):
                load_text_layer(sp, s, p, p)

        @blk.gpsimd
        def _(pool):
            pool.memset(X1[F:F + 1, :, :], 1.0).then_inc(g["tw_ready"], 1)
            pool.wait_ge(txt["ids_ready"], START + 1)
            for b in range(B):
                pool.indirect_dma_start(out=Hs[:, b * TPB + 2, :], out_offset=None, in_=a["L0_txt_emb"],
                                        in_offset=bass.IndirectOffsetOnAxis(ap=ids[:, b:b + 1], axis=0)).then_inc(txt["sw_emb"], 16)
            with pool.Fori(0, B) as t:
                pool.wait_ge(g["tvar_done"], START + t + 1)
                nc.gpsimd.tensor_tensor(out=RS[:], in0=VE[:], in1=K[:, C_NHALF:C_NHALF + 1].to_broadcast([P, 2]), op=ALU.pow).then_inc(g["trstd_done"], 1)

        @blk.tensor
        def _(pe):
            pe.wait_ge(g["tw_load"], START + 16 * 24)
            for i in range(3):
                last = nc.tensor.transpose(ps[0:F, 0, i * F:(i + 1) * F], wraw[:, i, :], ident[0:F, 0:F])
            last.then_inc(g["tw_tr"], 1)
            pe.wait_ge(g["tw_exp"], START + 1)
            for sc in range(2):
                for tc in range(2):
                    last = nc.tensor.transpose(ps[:, 1, sc * 256 + tc * P:sc * 256 + (tc + 1) * P], wb[:, tc, sc * P:(sc + 1) * P], ident)
            last.then_inc(g["tw_tr"], 1)
            pe.wait_ge(g["tw_ready"], START + 1 + 6)
            with pe.Fori(0, B // 2) as tp:
                for u in range(2):
                    t = tp * 2 + u
                    pe.wait_ge(g[f"x_loaded{u}"], START + tp * 16 + 16)
                    for lt in range(2):
                        pe.wait_ge(g["ekv_done"], START + 2 * t + lt - 1)
                        xv = X1[:, u, :].rearrange("c (l h) -> c h l", h=HT)
                        for h in range(HT):
                            last = nc.tensor.matmul(ps[:, 2 * lt + h // 2, (h % 2) * 256:(h % 2) * 256 + 256],
                                                    xv[:, h, lt * P:(lt + 1) * P], WT[:, h, :], start=True, stop=True)
                        last.then_inc(g["proj_done"], 1)
                    pe.wait_ge(g["ekv_done"], START + 2 * t + 2)
                    for tt in range(2):
                        pe.wait_ge(g["y_done"], START + 2 * t + tt - 1)
                        for sc in range(2):
                            last = nc.tensor.matmul(ps[:, 4 + tt, :], ewT[:, sc, tt * P:(tt + 1) * P], EK[:, u, sc, :],
                                                    start=(sc == 0), stop=(sc == 1))
                        last.then_inc(g["mix_done"], 1)
                    for tt in range(2):
                        pe.wait_ge(g["y_done"], START + 2 * t + tt + 1)
                        pe.wait_ge(g["yt_done"], START + 2 * t + tt)
                        for c in range(DC):
                            last = nc.tensor.transpose(ps[:, 6, c * P:(c + 1) * P], Y[:, tt, c * P:(c + 1) * P], ident)
                        last.then_inc(g["yt_tr"], 1)
                    for tt in range(2):
                        pe.wait_ge(g["yt_done"], START + 2 * t + tt + 1)
                        pe.wait_ge(g["tz_scaled"], START + 2 * t + tt)
                        for c in range(DC):
                            last = nc.tensor.matmul(ps[:, 7, 0:D], YT[:, tt, c, :], ow[:, c, :], start=(c == 0), stop=(c == DC - 1))
                        last.then_inc(g["o_done"], 1)

        @blk.scalar
        def _(act):
            act.wait_ge(g["tw_mask"], START + 1)
            nc.scalar.activation(wb[:], wb[:], ACT.Exp).then_inc(g["tw_exp"], 1)
            with act.Fori(0, B // 2) as tp:
                for u in range(2):
                    t = tp * 2 + u
                    act.wait_ge(g["mix_done"], START + 2 * t - 2)
                    act.wait_ge(g["tok_out"], START + 2 * t - 2)
                    for lt in range(2):
                        act.wait_ge(g["proj_done"], START + 2 * t + lt + 1)
                        v = ps[:, 2 * lt:2 * lt + 2, :].rearrange("p b (h f) -> p (b h) f", f=256)
                        nc.scalar.activation(EK[:, u, lt, D:2 * D].rearrange("p (h f) -> p h f", f=F), v[:, :, F:2 * F], ACT.Exp)
                        nc.scalar.activation(EQ[:, u, lt, :].rearrange("p (h f) -> p h f", f=F), v[:, :, 0:F], ACT.Exp, scale=-1.0)
                        nc.scalar.activation(XR[:, u, lt, :].rearrange("p (h f) -> p h f", f=F), v[:, :, 3 * F:4 * F], ACT.Copy).then_inc(g["tokact_done"], 1)
                    for tt in range(2):
                        act.wait_ge(g["yt_tr"], START + 2 * t + tt + 1)
                        nc.scalar.activation(YT[:, tt, :, :].rearrange("p c n -> p (c n)"), ps[:, 6, 0:D], ACT.Copy).then_inc(g["yt_done"], 1)

        @blk.vector
        def _(dve):
            ic = Chain(dve, txt["ids_chain"])
            dve.wait_ge(txt["ids_loaded"], START + 16)
            ic.link(nc.vector.tensor_copy(idf[:], ids[:]))
            ic.link(nc.vector.tensor_scalar(out=idn[:], in0=idf[:], scalar1=0.0, scalar2=float(VOCAB), op0=ALU.is_lt, op1=ALU.mult))
            ic.link(nc.vector.tensor_tensor(out=idf[:], in0=idf[:], in1=idn[:], op=ALU.add))
            ic.link(nc.vector.tensor_scalar(out=idf[:], in0=idf[:], scalar1=0.0, scalar2=float(VOCAB - 1), op0=ALU.max, op1=ALU.min))
            nc.vector.tensor_copy(ids[:], idf[:]).then_inc(txt["ids_ready"], 1)
            ch = Chain(dve, g["tok_chain"])
            dve.wait_ge(g["tw_load"], START + 16 * 24)
            nc.vector.tensor_tensor(out=wb[:], in0=wb[:], in1=msk[:].bitcast(U8), op=ALU.mult).then_inc(g["tw_mask"], 1)
            dve.wait_ge(g["tw_tr"], START + 1)
            for h in range(HT):
                nc.vector.tensor_copy(WT[0:F, h, 0:3 * F], ps[0:F, 0, 0:3 * F]).then_inc(g["tw_ready"], 1)
            nc.vector.tensor_copy(WT[0:F, :, 3 * F:], ident[0:F, None, 0:F].to_broadcast([F, HT, F])).then_inc(g["tw_ready"], 1)
            dve.wait_ge(g["tw_tr"], START + 2)
            nc.vector.tensor_copy(ewT[:].rearrange("p c n -> p (c n)"), ps[:, 1, :]).then_inc(g["tw_ready"], 1)
            PER = 14
            with dve.Fori(0, B // 2) as tp:
                for u in range(2):
                    t = tp * 2 + u
                    ch.begin(t * PER)
                    for lt in range(2):
                        dve.wait_ge(g["tokact_done"], START + 2 * t + lt + 1)
                        v = ps[:, 2 * lt:2 * lt + 2, :].rearrange("p b (h f) -> p (b h) f", f=256)
                        nc.vector.tensor_tensor(out=EK[:, u, lt, 0:D].rearrange("p (h f) -> p h f", f=F), in0=v[:, :, 2 * F:3 * F],
                                                in1=EK[:, u, lt, D:2 * D].rearrange("p (h f) -> p h f", f=F), op=ALU.mult).then_inc(g["ekv_done"], 1)
                    for tt in range(2):
                        dve.wait_ge(g["mix_done"], START + 2 * t + tt + 1)
                        ch.link(nc.vector.scalar_tensor_tensor(out=DEN[:, tt, :], in0=EQ[:, u, tt, :], scalar=1.0, in1=ps[:, 4 + tt, D:2 * D], op0=ALU.add, op1=ALU.mult))
                        ch.link(nc.vector.reciprocal(DEN[:, tt, :], DEN[:, tt, :]))
                        nc.vector.tensor_tensor(out=Y[:, tt, :], in0=ps[:, 4 + tt, 0:D], in1=DEN[:, tt, :], op=ALU.mult).then_inc(g["y_done"], 1)
                    for tt in range(2):
                        dve.wait_ge(g["o_done"], START + 2 * t + tt + 1)
                        nc.vector.tensor_tensor(out=Z[:, tt, :], in0=ps[:, 7, 0:D], in1=XR[:, u, tt, :], op=ALU.add).then_inc(g["tz_scaled"], 1)
                        dve.wait_ge(g["tz_scaled"], START + 2 * t + tt + 1)
                        ch.link(nc.vector.bn_stats(ST[:, tt, :], Z[:, tt, :]))
                        dve.sem_inc(g["waited"], 1)
                        ch.link(nc.vector.bn_aggr(MV[:, tt, :], ST[:, tt, :]))
                    nc.vector.tensor_scalar(out=VE[:], in0=MV[:, :, 1], scalar1=EPS, scalar2=None, op0=ALU.add).then_inc(g["tvar_done"], 1)
                    dve.wait_ge(g["trstd_done"], START + t + 1)
                    for tt in range(2):
                        ch.link(nc.vector.tensor_scalar(out=Z[:, tt, :], in0=Z[:, tt, :], scalar1=MV[:, tt, 0:1], scalar2=RS[:, tt:tt + 1], op0=ALU.subtract, op1=ALU.mult))
                        ch.link(nc.vector.tensor_tensor(out=Z[:, tt, :], in0=Z[:, tt, :], in1=gb[:, 0, :], op=ALU.mult))
                        ch.link(nc.vector.tensor_tensor(out=Hs[:, bass.ds(t * TPB + tt, 1), :].rearrange("p o d -> p (o d)"), in0=Z[:, tt, :], in1=gb[:, 1, :], op=ALU.add))
                        nc.vector.sem_inc(g["tok_out"], 1)
                    ch.end(PER)


def txt_phase(s, made):
    sem = s["sem"]
    if made is None:
        names = ["ids_loaded", "ids_chain", "ids_ready", "sw_emb", "emb_ready", "v_rest", "w_loaded0", "w_loaded1", "h_tr", "ht_done",
                 "qk_mm", "v_mm", "q_done", "k_done", "v_done", "s_done", "max_done", "exp_done", "pt_tr", "v_hi", "pt_hi", "pt_rest", "pt_done", "pv_done",
                 "onorm_done", "ot_tr", "ot_done", "wc_done", "z1_done", "var1_done", "rstd1_done", "h1_done", "h1b_done",
                 "h1_tr", "h1t_done", "ff1_mm", "ff1_done", "ff2_done", "z2_done", "var2_done", "rstd2_done", "txt_out",
                 "txt_chain", "txt_waited"]
        return {n: sem(n) for n in names}
    g = made
    nc, a, K, ident, Hs, ps, sb = s["nc"], s["a"], s["K"], s["ident"], s["Hs"], s["ps"], s["sb"]
    G = 4
    W = s["txt_w"]
    hT = sb("hT", [P, DC, G * P])
    QT = sb("qT", [P, DC, G * P])
    K2 = sb("kT_masked", [P, DC, G, 2, P])
    V1 = sb("v_parts", [P, G, H, 3, KD], BF16)
    VR = sb("v_rest", [P, G, H, KD])
    PR = sb("probs", [P, 4, 4, P])
    NM = sb("neg_max", [P, 4, 4])
    PT = [sb(f"probsT_{x}", [P, 2, 4, P], BF16) for x in range(3)]
    PTR = sb("probsT_rest", [P, 2, 4, P])
    SUM = sb("prob_sums", [P, 2, 4, 4])
    RC = sb("recip", [P, H])
    OL = sb("heads_sum", [P, H, KD])
    O = sb("heads_out", [P, D])
    OT = sb("heads_outT", [P, DC, P])
    Z = sb("z1", [P, G, D])
    Z2 = sb("z2", [P, G, D])
    H1B = sb("h1_b2", [P, G, D])
    F1T = sb("ff1T", [P, MC, G * P])
    ST = sb("txt_st", [P, G, 6])
    MV = sb("txt_mv", [P, G, 2])
    VE = sb("txt_ve", [P, G])
    RS = sb("txt_rs", [P, G])
    h1T = hT

    def heads_of(bank, slot):
        return (slot // 2) * 8 + bank * 2 + slot % 2

    blk = nc.Block()
    with blk:
        @blk.sync
        def _(sp):
            load_attn(sp, s)
            with sp.Fori(1, LAYERS // 2) as lp:
                for p in range(2):
                    sp.wait_ge(g["txt_out"], START + B * (lp * 2 + p) - B)
                    load_text_layer(sp, s, lp * 2 + p, p)

        @blk.gpsimd
        def _(pool):
            with pool.Fori(0, LAYERS // 2) as lp:
                for p in range(2):
                    pool.wait_ge(g[f"w_loaded{p}"], START + 192 * lp + 192)
                    for hf in range(2):
                        q = lp * 4 + p * 2 + hf
                        half = K[:, C_NHALF:C_NHALF + 1].to_broadcast([P, G])
                        pool.wait_ge(g["z2_done"], START + q * G)
                        for j in range(G):
                            pool.wait_ge(g["var1_done"], START + q * G + j + 1)
                            nc.gpsimd.tensor_tensor(out=RS[:, j:j + 1], in0=VE[:, j:j + 1], in1=K[:, C_NHALF:C_NHALF + 1], op=ALU.pow).then_inc(g["rstd1_done"], 1)
                            pool.wait_ge(g["h1_done"], START + q * G + j + 1)
                            nc.gpsimd.tensor_tensor(out=H1B[:, j, :], in0=Z[:, j, :], in1=W[p]["vec"][:, 0, :], op=ALU.add).then_inc(g["h1b_done"], 1)
                        pool.wait_ge(g["var2_done"], START + q + 1)
                        nc.gpsimd.tensor_tensor(out=RS[:], in0=VE[:], in1=half, op=ALU.pow).then_inc(g["rstd2_done"], 1)

        @blk.tensor
        def _(pe):
            pe.wait_ge(g["emb_ready"], START + 1)
            with pe.Fori(0, LAYERS // 2) as lp:
                for p in range(2):
                    w = W[p]
                    pe.wait_ge(g[f"w_loaded{p}"], START + 192 * lp + 192)
                    for hf in range(2):
                        q = lp * 4 + p * 2 + hf
                        T = q * G

                        def transpose_group(name, src, count):
                            for c in range(DC):
                                for j in range(G):
                                    if c == 0:
                                        pe.wait_ge(g[count], START + T + j + 1)
                                    last = nc.tensor.transpose(ps[:, 4 + c, j * P:(j + 1) * P], src(j, c), ident)
                                last.then_inc(g[name], 1)

                        pe.wait_ge(g["txt_out"], START + T - G)
                        pe.wait_ge(g["h1t_done"], START + 2 * q)
                        for c in range(DC):
                            for j in range(G):
                                tile = hf * (G * TPB) + (j * TPB + 2)
                                last = nc.tensor.transpose(ps[:, 4 + c, j * P:(j + 1) * P],
                                                           Hst(Hs, tile, c), ident)
                            last.then_inc(g["h_tr"], 1)
                        pe.wait_ge(g["ht_done"], START + 2 * q + 2)
                        for i in range(2):
                            for dc in range(DC):
                                for c in range(DC):
                                    last = nc.tensor.matmul(ps[:, 2 * i + dc, :], w["qkv"][:, c, i, dc * P:(dc + 1) * P], hT[:, c, :],
                                                            start=(c == 0), stop=(c == DC - 1))
                                last.then_inc(g["qk_mm"], 1)
                        pe.wait_ge(g["z2_done"], START + T)
                        for j in range(G):
                            for c in range(DC):
                                last = nc.tensor.matmul(ps[:, 6 + j // 2, (j % 2) * D:(j % 2) * D + D], hT[:, c, j * P:(j + 1) * P], w["qkv"][:, c, 2, :],
                                                        start=(c == 0), stop=(c == DC - 1))
                            last.then_inc(g["v_mm"], 1)
                        pe.wait_ge(g["q_done"], START + 2 * q + 2)
                        pe.wait_ge(g["k_done"], START + 2 * q + 2)

                        def scores(j, b):
                            n = T * 4 + (4 * j + b)
                            if j > 0:
                                pe.wait_ge(g["exp_done"], START + n - 3)
                            for c in range(DC):
                                last = nc.tensor.matmul(ps[:, b, c * 256:(c + 1) * 256], QT[32 * b:32 * b + 32, c, j * P:(j + 1) * P],
                                                        K2[32 * b:32 * b + 32, c, j, :, :].rearrange("p e l -> p (e l)"), start=True, stop=True)
                            last.then_inc(g["s_done"], 1)

                        def probs_transpose(j, b):
                            n = T * 4 + (4 * j + b)
                            pe.wait_ge(g["exp_done"], START + n + 1)
                            pe.wait_ge(g["pt_rest"], START + n - 1)
                            for i in range(4):
                                last = nc.tensor.transpose(ps[:, 4 + b % 2, i * P:(i + 1) * P], PR[:, b, i, :], ident)
                            last.then_inc(g["pt_tr"], 1)

                        def values(j, b):
                            n = T * 4 + (4 * j + b)
                            pe.wait_ge(g["pt_done"], START + n + 1)
                            if b == 0:
                                pe.wait_ge(g["v_done"], START + q + 1)
                                pe.wait_ge(g["onorm_done"], START + T + j)
                            for i in range(4):
                                h = heads_of(b, i)
                                at = h * 2 * KD
                                v12 = V1[:, j, h, 0:2, :].rearrange("p x k -> p (x k)")
                                nc.tensor.matmul(ps[:, 6, at:at + 2 * KD], PT[0][:, b % 2, i, :], v12, start=True, stop=True)
                                nc.tensor.matmul(ps[:, 6, at:at + KD], PT[0][:, b % 2, i, :], V1[:, j, h, 2, :], start=False, stop=True, skip_group_check=True)
                                nc.tensor.matmul(ps[:, 6, at:at + 2 * KD], PT[1][:, b % 2, i, :], v12, start=False, stop=True, skip_group_check=True)
                                last = nc.tensor.matmul(ps[:, 6, at:at + 2 * KD], PT[2][:, b % 2, i, :], v12, start=False, stop=True, skip_group_check=True)
                            last.then_inc(g["pv_done"], 1)

                        def out_transpose(j):
                            pe.wait_ge(g["onorm_done"], START + T + j + 1)
                            pe.wait_ge(g["z1_done"], START + T + j)
                            for c in range(DC):
                                last = nc.tensor.transpose(ps[:, 7, c * P:(c + 1) * P], O[:, c * P:(c + 1) * P], ident)
                            last.then_inc(g["ot_tr"], 1)

                        def out_project(j):
                            pe.wait_ge(g["ot_done"], START + T + j + 1)
                            for c in range(DC):
                                last = nc.tensor.matmul(ps[:, 7, D:2 * D], OT[:, c, :], w["wc"][:, c, :], start=(c == 0), stop=(c == DC - 1))
                            last.then_inc(g["wc_done"], 1)

                        for b in range(4):
                            scores(0, b)
                        for j in range(G):
                            for b in range(4):
                                if j + 1 < G:
                                    scores(j + 1, b)
                                probs_transpose(j, b)
                                if b > 0:
                                    values(j, b - 1)
                                elif j > 0:
                                    values(j - 1, 3)
                                if j > 0 and b == 1:
                                    out_transpose(j - 1)
                                if j > 0 and b == 3:
                                    out_project(j - 1)
                        values(G - 1, 3)
                        out_transpose(G - 1)
                        out_project(G - 1)

                        transpose_group("h1_tr", lambda j, c: Z[:, j, c * P:(c + 1) * P], "h1_done")
                        pe.wait_ge(g["h1t_done"], START + 2 * q + 2)
                        for m in range(MC):
                            pe.wait_ge(g["ff1_done"], START + q * MC + m - 3)
                            for c in range(DC):
                                last = nc.tensor.matmul(ps[:, m % 4, :], w["w1"][:, c, m * P:(m + 1) * P], h1T[:, c, :], start=(c == 0), stop=(c == DC - 1))
                            last.then_inc(g["ff1_mm"], 1)
                        pe.wait_ge(g["ff1_done"], START + q * MC + MC)
                        for j in range(G):
                            pe.wait_ge(g["z2_done"], START + T + j - 1)
                            for m in range(MC):
                                last = nc.tensor.matmul(ps[:, 6 + j % 2, 0:D], F1T[:, m, j * P:(j + 1) * P], w["w2"][:, m, :], start=(m == 0), stop=(m == MC - 1))
                            last.then_inc(g["ff2_done"], 1)

        @blk.scalar
        def _(act):
            with act.Fori(0, LAYERS // 2) as lp:
                for p in range(2):
                    w = W[p]
                    act.wait_ge(g[f"w_loaded{p}"], START + 192 * lp + 192)
                    for hf in range(2):
                        q = lp * 4 + p * 2 + hf
                        T = q * G
                        act.wait_ge(g["ff1_mm"], START + q * MC)
                        for c in range(DC):
                            act.wait_ge(g["h_tr"], START + 2 * q + (c + 1))
                            nc.scalar.activation(hT[:, c, :], ps[:, 4 + c, :], ACT.Copy).then_inc(g["ht_done"], 1)
                        for dc in range(DC):
                            act.wait_ge(g["qk_mm"], START + 4 * q + dc + 1)
                            nc.scalar.activation(QT[:, dc, :], ps[:, dc, :], ACT.Copy, scale=float(KD) ** -0.5).then_inc(g["q_done"], 1)
                        for j in range(G):
                            act.wait_ge(g["v_mm"], START + T + (2 * (j // 2) + 2))
                            nc.scalar.activation(V1[:, j, :, 0, :], ps[:, 6 + j // 2, (j % 2) * D:(j % 2) * D + D].rearrange("p (h k) -> p h k", k=KD), ACT.Copy).then_inc(g["v_hi"], 1)

                        def out_copy(j):
                            act.wait_ge(g["ot_tr"], START + T + j + 1)
                            act.wait_ge(g["wc_done"], START + T + j)
                            nc.scalar.activation(OT[:].rearrange("p c n -> p (c n)"), ps[:, 7, 0:D], ACT.Copy).then_inc(g["ot_done"], 1)

                        for j in range(G):
                            for b in range(4):
                                n = T * 4 + (4 * j + b)
                                act.wait_ge(g["max_done"], START + n + 1)
                                act.wait_ge(g["pt_tr"], START + n - 3)
                                act.wait_ge(g["onorm_done"], START + T + j - 1)
                                for i in range(4):
                                    last = nc.scalar.activation(PR[:, b, i, :], ps[:, b, i * P:(i + 1) * P], ACT.Exp, bias=NM[:, b, i:i + 1],
                                                                accum_out=SUM[:, j % 2, b, i:i + 1])
                                last.then_inc(g["exp_done"], 1)
                                if j > 0 and b == 2:
                                    out_copy(j - 1)
                        out_copy(G - 1)
                        for c in range(DC):
                            act.wait_ge(g["h1_tr"], START + 2 * q + (c + 1))
                            nc.scalar.activation(h1T[:, c, :], ps[:, 4 + c, :], ACT.Copy).then_inc(g["h1t_done"], 1)
                        act.wait_ge(g["ff2_done"], START + T)
                        for m in range(MC):
                            act.wait_ge(g["ff1_mm"], START + q * MC + m + 1)
                            nc.scalar.activation(F1T[:, m, :], ps[:, m % 4, :], ACT.Relu, bias=w["b1"][:, m:m + 1]).then_inc(g["ff1_done"], 1)

        @blk.vector
        def _(dve):
            dve.wait_ge(g["sw_emb"], 16 * B)
            hv = Hs[:].rearrange("p (b t) d -> p b t d", t=TPB)[:, :, TPB - 1, :]
            nc.vector.tensor_tensor(out=hv, in0=hv, in1=K[:, None, C_PE:C_PE + D].to_broadcast([P, B, D]), op=ALU.add).then_inc(g["emb_ready"], 1)
            ch = Chain(dve, g["txt_chain"])
            PER = 41
            with dve.Fori(0, LAYERS // 2) as lp:
                for p in range(2):
                    w = W[p]
                    b2, g1, be1, g2, be2 = (w["vec"][:, i, :] for i in range(5))
                    dve.wait_ge(g[f"w_loaded{p}"], START + 192 * lp + 192)
                    for hf in range(2):
                        q = lp * 4 + p * 2 + hf
                        T = q * G
                        ch.begin(q * PER)
                        for dc in range(DC):
                            dve.wait_ge(g["qk_mm"], START + 4 * q + (2 + dc + 1))
                            kt = ps[:, 2 + dc, :].rearrange("p (g l) -> p g l", g=G)
                            nc.vector.tensor_scalar(out=K2[:, dc, :, 0, :], in0=kt, scalar1=K[:, C_EO:C_EO + 1], scalar2=None, op0=ALU.mult)
                            nc.vector.tensor_scalar(out=K2[:, dc, :, 1, :], in0=kt, scalar1=K[:, C_EO + 1:C_EO + 2], scalar2=None, op0=ALU.mult).then_inc(g["k_done"], 1)

                        for j in range(G):
                            dve.wait_ge(g["v_hi"], START + T + (2 * (j // 2) + 2))
                            nc.vector.tensor_tensor(out=VR[:, j, :, :], in0=ps[:, 6 + j // 2, (j % 2) * D:(j % 2) * D + D].rearrange("p (h k) -> p h k", k=KD),
                                                    in1=V1[:, j, :, 0, :], op=ALU.subtract).then_inc(g["v_rest"], 1)
                        def row_max(j, b):
                            n = T * 4 + (4 * j + b)
                            dve.wait_ge(g["s_done"], START + n + 1)
                            dve.wait_ge(g["exp_done"], START + n - 3)
                            nc.vector.tensor_reduce(out=NM[:, b, :], in_=ps[:, b, :].rearrange("p (i l) -> p i l", i=4), op=ALU.max, axis=AX.X, negate=True).then_inc(g["max_done"], 1)

                        def probs_copy(j, b):
                            n = T * 4 + (4 * j + b)
                            dve.wait_ge(g["pt_tr"], START + n + 1)
                            dve.wait_ge(g["pv_done"], START + n - 1)
                            p1, p2, p3, rest = (x[:, b % 2, :, :].rearrange("p i l -> p (i l)") for x in (*PT, PTR))
                            nc.vector.tensor_copy(p1, ps[:, 4 + b % 2, :]).then_inc(g["pt_hi"], 1)
                            dve.wait_ge(g["pt_hi"], START + 2 * n + 1)
                            nc.vector.tensor_tensor(out=rest, in0=ps[:, 4 + b % 2, :], in1=p1, op=ALU.subtract).then_inc(g["pt_rest"], 1)
                            dve.wait_ge(g["pt_rest"], START + n + 1)
                            nc.vector.tensor_copy(p2, rest).then_inc(g["pt_hi"], 1)
                            dve.wait_ge(g["pt_hi"], START + 2 * n + 2)
                            nc.vector.tensor_tensor(out=p3, in0=rest, in1=p2, op=ALU.subtract).then_inc(g["pt_done"], 1)

                        def normalise(j):
                            dve.wait_ge(g["pv_done"], START + T * 4 + 4 * (j + 1))
                            dve.wait_ge(g["ot_tr"], START + T + j)
                            nc.vector.reciprocal(RC[:].rearrange("p (c b e) -> p b c e", c=DC, b=4), SUM[:, j % 2, :, :].rearrange("p b (c e) -> p b c e", c=DC))
                            ov = ps[:, 6, :].rearrange("p (h x k) -> p h x k", x=2, k=KD)
                            Ov = O[:].rearrange("p (h k) -> p h k", k=KD)
                            ch.link(nc.vector.tensor_copy(OL[:], ov[:, :, 1, :]))
                            ch.link(nc.vector.tensor_tensor(out=OL[:], in0=ov[:, :, 0, :], in1=OL[:], op=ALU.add))
                            nc.vector.tensor_tensor(out=Ov, in0=OL[:], in1=RC[:, :, None].to_broadcast([P, H, KD]), op=ALU.mult).then_inc(g["onorm_done"], 1)

                        def stats(z, j):
                            ch.link(nc.vector.bn_stats(ST[:, j, :], z))
                            dve.sem_inc(g["txt_waited"], 1)
                            ch.link(nc.vector.bn_aggr(MV[:, j, :], ST[:, j, :]))

                        def residual1(j):
                            dve.wait_ge(g["wc_done"], START + T + j + 1)
                            tile = hf * (G * TPB) + (j * TPB + 2)
                            nc.vector.tensor_tensor(out=Z[:, j, :], in0=ps[:, 7, D:2 * D], in1=Hst(Hs, tile), op=ALU.add).then_inc(g["z1_done"], 1)
                            dve.wait_ge(g["z1_done"], START + T + j + 1)
                            stats(Z[:, j, :], j)
                            nc.vector.tensor_scalar(out=VE[:, j:j + 1], in0=MV[:, j, 1:2], scalar1=EPS, scalar2=None, op0=ALU.add).then_inc(g["var1_done"], 1)

                        def norm1(j):
                            dve.wait_ge(g["rstd1_done"], START + T + j + 1)
                            norm(Z[:, j, :], j, g1, be1, Z[:, j, :], "h1_done")

                        def norm(z, j, ga, be, to, count):
                            ch.link(nc.vector.tensor_scalar(out=z, in0=z, scalar1=MV[:, j, 0:1], scalar2=RS[:, j:j + 1], op0=ALU.subtract, op1=ALU.mult))
                            ch.link(nc.vector.tensor_tensor(out=z, in0=z, in1=ga, op=ALU.mult))
                            nc.vector.tensor_tensor(out=to, in0=z, in1=be, op=ALU.add).then_inc(g[count], 1)

                        for b in range(4):
                            row_max(0, b)
                        dve.wait_ge(g["v_rest"], START + T + G)
                        ch.link(nc.vector.tensor_copy(V1[:, :, :, 1, :].rearrange("p g h k -> p (g h) k"), VR[:].rearrange("p g h k -> p (g h) k")))
                        nc.vector.tensor_tensor(out=V1[:, :, :, 2, :].rearrange("p g h k -> p (g h) k"), in0=VR[:].rearrange("p g h k -> p (g h) k"),
                                                in1=V1[:, :, :, 1, :].rearrange("p g h k -> p (g h) k"), op=ALU.subtract).then_inc(g["v_done"], 1)
                        dve.wait_ge(g["h1b_done"], START + T)
                        for j in range(G):
                            for b in range(4):
                                if j + 1 < G:
                                    row_max(j + 1, b)
                                probs_copy(j, b)
                                if j > 0 and b == 0:
                                    normalise(j - 1)
                                if j > 1 and b == 0:
                                    residual1(j - 2)
                                if j > 1 and b == 2:
                                    norm1(j - 2)
                        normalise(G - 1)
                        residual1(G - 2)
                        norm1(G - 2)
                        residual1(G - 1)
                        norm1(G - 1)
                        for j in range(G):
                            dve.wait_ge(g["ff2_done"], START + T + j + 1)
                            dve.wait_ge(g["h1b_done"], START + T + j + 1)
                            nc.vector.tensor_tensor(out=Z2[:, j, :], in0=ps[:, 6 + j % 2, 0:D], in1=H1B[:, j, :], op=ALU.add).then_inc(g["z2_done"], 1)
                            dve.wait_ge(g["z2_done"], START + T + j + 1)
                            stats(Z2[:, j, :], j)
                        nc.vector.tensor_scalar(out=VE[:], in0=MV[:, :, 1], scalar1=EPS, scalar2=None, op0=ALU.add).then_inc(g["var2_done"], 1)
                        dve.wait_ge(g["rstd2_done"], START + q + 1)
                        for j in range(G):
                            tile = hf * (G * TPB) + (j * TPB + 2)
                            norm(Z2[:, j, :], j, g2, be2, Hst(Hs, tile), "txt_out")
                        ch.end(PER)


def attn_phase(s, made):
    sem = s["sem"]
    if made is None:
        names = ["aw_load", "wqT_tr", "wqT_done", "fold_mm", "aw_ready", "aw_rep", "avar_done", "arstd_done", "u_done", "gt_tr", "gt_done",
                 "aproj_done", "kv_done", "max1_done", "exp1_done", "wq_done", "cum1_done", "m_done", "t2_tr", "mt_done", "klog_done",
                 "kl_done", "max2_done", "exp2_done", "kw_done", "cum2_done", "attn_out", "attn_chain", "attn_waited"]
        return {n: sem(n) for n in names}
    g = made
    nc, a, K, ident, Hs, ps, sb = s["nc"], s["a"], s["K"], s["ident"], s["Hs"], s["ps"], s["sb"]
    tri, ones = s["tri"], s["ones"]
    W, WKA, WQA, BI, BKA, COL = (s["attn_w"][x] for x in ("W", "WKA", "WQA", "BI", "BKA", "COL"))
    WQT = sb("a_wqT", [P, DC, D])
    BQR = sb("a_bq_rep", [P, DC, P])
    U = sb("a_u", [P, 2, TPB, D])
    GT = sb("a_gT", [P, TPB, DC, P])
    QA = sb("a_qa", [P, 2, TPB, 2, D])
    KV = sb("a_kv", [P, 2, TPB, 2, D])
    WQ = sb("a_weighted_q", [P, TPB, D])
    Mx = sb("a_mixed", [P, TPB, D])
    MT = sb("a_mixedT", [P, TPB, DC, P])
    KL = sb("a_klog", [P, TPB, D])
    KW = sb("a_weighted_k", [P, TPB, D])
    TM = sb("a_tmp", [P, TPB, D])
    ST = sb("a_st", [P, TPB, 6])
    MV = sb("a_mv", [P, TPB, 2])
    VE = sb("a_ve", [P, TPB])
    RS = sb("a_rs", [P, TPB])
    NM = sb("a_negmax", [P, 2, TPB])
    SM = sb("a_sum", [P, 2, TPB])
    SCALE = float(D) ** -0.5

    def turn_bank(u, use):
        return (3, 5)[(u + use) % 2]

    def steps(eng, before, body):
        before()
        with eng.Fori(0, B // 2 - 1) as bp:
            for u in range(2):
                body(bp * 2 + u, u, None)
        for b in (B - 2, B - 1):
            body(b, b % 2, b)

    blk = nc.Block()
    with blk:
        @blk.gpsimd
        def _(pool):
            with pool.Fori(0, B) as b:
                pool.wait_ge(g["avar_done"], START + b + 1)
                nc.gpsimd.tensor_tensor(out=RS[:], in0=VE[:], in1=K[:, C_NHALF:C_NHALF + 1].to_broadcast([P, TPB]), op=ALU.pow).then_inc(g["arstd_done"], 1)

        @blk.tensor
        def _(pe):
            pe.wait_ge(g["aw_load"], START + 16 * 13)
            for mc in range(DC):
                for c in range(DC):
                    last = nc.tensor.transpose(ps[:, 0, mc * D + c * P:mc * D + (c + 1) * P], W[:, c, 0, mc * P:(mc + 1) * P], ident)
            last.then_inc(g["wqT_tr"], 1)
            pe.wait_ge(g["wqT_done"], START + 1)
            for c in range(DC):
                for mc in range(DC):
                    last = nc.tensor.matmul(ps[:, 1, c * D:(c + 1) * D], WQT[:, mc, c * P:(c + 1) * P], WQA[:, mc, :], start=(mc == 0), stop=(mc == DC - 1))
            last.then_inc(g["fold_mm"], 1)
            pe.wait_ge(g["aw_rep"], START + 2)
            for mc in range(DC):
                last = nc.tensor.matmul(ps[:, 2, 0:D], BQR[:, mc, :], WQA[:, mc, :], start=(mc == 0), stop=(mc == DC - 1))
            last.then_inc(g["fold_mm"], 1)
            pe.wait_ge(g["aw_ready"], START + 4)

            def rows_to_columns(b, u, j):
                n = b * TPB + j
                pe.wait_ge(g["u_done"], START + n + 1)
                pe.wait_ge(g["gt_done"], START + n)
                for c in range(DC):
                    last = nc.tensor.transpose(ps[:, 2, c * P:(c + 1) * P], U[:, u, j, c * P:(c + 1) * P], ident)
                last.then_inc(g["gt_tr"], 1)

            def project(b, j):
                n = b * TPB + j
                pe.wait_ge(g["gt_done"], START + n + 1)
                pe.wait_ge(g["kv_done"], START + n - min(j, 1))
                for i in range(2):
                    for c in range(DC):
                        last = nc.tensor.matmul(ps[:, (6 if j == 1 else 0) + i, :], GT[:, j, c, :], W[:, c, 2 * i:2 * i + 2, :].rearrange("p i n -> p (i n)"), start=(c == 0), stop=(c == DC - 1))
                last.then_inc(g["aproj_done"], 1)

            def running_sum(b, j, bank, src, ready):
                pe.wait_ge(g[ready], START + b * TPB + j + 1)
                for i in range(j):
                    nc.tensor.matmul(ps[:, bank, 0:D], ones, src[:, i, :], start=(i == 0), stop=False)
                return nc.tensor.matmul(ps[:, bank, 0:D], tri, src[:, j, :], start=(j == 0), stop=True)

            def mixed_transpose(b, j):
                n = b * TPB + j
                pe.wait_ge(g["m_done"], START + n + 1)
                pe.wait_ge(g["mt_done"], START + n)
                for c in range(DC):
                    last = nc.tensor.transpose(ps[:, 4, c * P:(c + 1) * P], Mx[:, j, c * P:(c + 1) * P], ident)
                last.then_inc(g["t2_tr"], 1)

            def query_sum(b, u, j):
                if j < 2:
                    pe.wait_ge(g["attn_out"], START + b * TPB - 1 + j)
                else:
                    pe.wait_ge(g["m_done"], START + b * TPB + 1)
                running_sum(b, j, turn_bank(u, j), WQ, "wq_done").then_inc(g["cum1_done"], 1)

            def key_logits(b, u, j):
                pe.wait_ge(g["mt_done"], START + b * TPB + j + 1)
                if j < 2:
                    pe.wait_ge(g["m_done"], START + b * TPB + j + 2)
                else:
                    pe.wait_ge(g["kl_done"], START + b * TPB + 1)
                for c in range(DC):
                    last = nc.tensor.matmul(ps[:, turn_bank(u, TPB + j), 0:D], MT[:, j, c, :], WKA[:, c, :], start=(c == 0), stop=(c == DC - 1))
                last.then_inc(g["klog_done"], 1)

            def key_sum(b, u, j):
                if j < 2:
                    pe.wait_ge(g["kl_done"], START + b * TPB + j + 2)
                else:
                    pe.wait_ge(g["attn_out"], START + b * TPB + 1)
                running_sum(b, j, turn_bank(u, 2 * TPB + j), KW, "kw_done").then_inc(g["cum2_done"], 1)

            def body(b, u, fixed):
                more = fixed is None or fixed < B - 1
                if more:
                    rows_to_columns(b + 1, 1 - u, 0)
                    rows_to_columns(b + 1, 1 - u, 1)
                    project(b + 1, 0)
                for j in range(TPB):
                    query_sum(b, u, j)
                if more:
                    rows_to_columns(b + 1, 1 - u, 2)
                for j in range(TPB):
                    mixed_transpose(b, j)
                    if j == 0 and more:
                        project(b + 1, 1)
                for j in range(TPB):
                    key_logits(b, u, j)
                if more:
                    project(b + 1, 2)
                for j in range(TPB):
                    key_sum(b, u, j)

            def before():
                for j in range(TPB):
                    rows_to_columns(0, 0, j)
                for j in range(TPB):
                    project(0, j)

            steps(pe, before, body)

        @blk.scalar
        def _(act):
            act.wait_ge(g["wqT_tr"], START + 1)
            nc.scalar.activation(WQT[:].rearrange("p c n -> p (c n)"), ps[:, 0, :], ACT.Copy).then_inc(g["wqT_done"], 1)

            def columns_out(b, j):
                n = b * TPB + j
                act.wait_ge(g["gt_tr"], START + n + 1)
                act.wait_ge(g["aproj_done"], START + n - 2)
                for c in range(DC):
                    last = nc.scalar.activation(GT[:, j, c, :], ps[:, 2, c * P:(c + 1) * P], ACT.Identity, scale=COL[:, 0, c:c + 1], bias=COL[:, 1, c:c + 1])
                last.then_inc(g["gt_done"], 1)

            def softmax(b, j, i, src, ready, count):
                act.wait_ge(g[ready], START + b * TPB + j + 1)
                nc.scalar.activation(src, src, ACT.Exp, bias=NM[:, i, j:j + 1], accum_out=SM[:, i, j:j + 1]).then_inc(g[count], 1)

            def body(b, u, fixed):
                more = fixed is None or fixed < B - 1
                if more:
                    columns_out(b + 1, 0)
                    columns_out(b + 1, 1)
                for j in range(TPB):
                    softmax(b, j, 0, QA[:, u, j, 1, :], "max1_done", "exp1_done")
                if more:
                    columns_out(b + 1, 2)
                for j in range(TPB):
                    n = b * TPB + j
                    act.wait_ge(g["t2_tr"], START + n + 1)
                    act.wait_ge(g["klog_done"], START + n - 2)
                    nc.scalar.activation(MT[:, j, :, :].rearrange("p c n -> p (c n)"), ps[:, 4, 0:D], ACT.Copy).then_inc(g["mt_done"], 1)
                for j in range(TPB):
                    softmax(b, j, 1, KL[:, j, :], "max2_done", "exp2_done")

            def before():
                for j in range(TPB):
                    columns_out(0, j)

            steps(act, before, body)

        @blk.vector
        def _(dve):
            ch = Chain(dve, g["attn_chain"])
            dve.wait_ge(g["aw_load"], START + 16 * 13)
            for c in range(DC):
                nc.vector.tensor_scalar(out=BQR[:, c, :], in0=ones, scalar1=COL[:, 2, c:c + 1], scalar2=None, op0=ALU.mult).then_inc(g["aw_rep"], 1)
            dve.wait_ge(g["fold_mm"], START + 1)
            nc.vector.tensor_scalar(out=W[:, :, 1, :], in0=ps[:, 1, :].rearrange("p (c n) -> p c n", n=D), scalar1=SCALE, scalar2=None, op0=ALU.mult).then_inc(g["aw_ready"], 1)
            dve.wait_ge(g["fold_mm"], START + 2)
            ch.begin(0)
            ch.link(nc.vector.tensor_tensor(out=BI[:, 1, :], in0=ps[:, 2, 0:D], in1=BI[:, 1, :], op=ALU.add))
            nc.vector.tensor_scalar(out=BI[:, 1, :], in0=BI[:, 1, :], scalar1=SCALE, scalar2=None, op0=ALU.mult).then_inc(g["aw_ready"], 1)
            nc.vector.tensor_scalar(out=WKA[:], in0=WKA[:], scalar1=SCALE, scalar2=None, op0=ALU.mult).then_inc(g["aw_ready"], 1)
            nc.vector.tensor_scalar(out=BKA[:], in0=BKA[:], scalar1=SCALE, scalar2=None, op0=ALU.mult).then_inc(g["aw_ready"], 1)
            dve.wait_ge(g["aw_ready"], START + 4)
            PRE = 1

            def norm_rows(b, u):
                for j in range(TPB):
                    ch.link(nc.vector.bn_stats(ST[:, j, :], Hst(Hs, b * TPB + j)))
                    dve.sem_inc(g["attn_waited"], 1)
                    ch.link(nc.vector.bn_aggr(MV[:, j, :], ST[:, j, :]))
                nc.vector.tensor_scalar(out=VE[:], in0=MV[:, :, 1], scalar1=1.0 + EPS, scalar2=EPS * EPS, op0=ALU.mult, op1=ALU.add).then_inc(g["avar_done"], 1)
                dve.wait_ge(g["arstd_done"], START + b + 1)
                dve.wait_ge(g["gt_tr"], START + b * TPB - TPB)
                for j in range(TPB):
                    nc.vector.tensor_scalar(out=U[:, u, j, :], in0=Hst(Hs, b * TPB + j), scalar1=MV[:, j, 0:1], scalar2=RS[:, j:j + 1], op0=ALU.subtract, op1=ALU.mult).then_inc(g["u_done"], 1)

            def add_biases(b, u, j):
                k = 6 if j == 1 else 0
                dve.wait_ge(g["aproj_done"], START + b * TPB + j + 1)
                nc.vector.tensor_tensor(out=QA[:, u, j, :, :].rearrange("p i n -> p (i n)"), in0=ps[:, k, :], in1=BI[:, 0:2, :].rearrange("p i n -> p (i n)"), op=ALU.add)
                nc.vector.tensor_tensor(out=KV[:, u, j, :, :].rearrange("p i n -> p (i n)"), in0=ps[:, k + 1, :], in1=BI[:, 2:4, :].rearrange("p i n -> p (i n)"), op=ALU.add).then_inc(g["kv_done"], 1)

            def out_stats(b, j):
                n = b * TPB + j
                dve.wait_ge(g["attn_out"], START + n + 1)
                nc.vector.bn_stats(s["out_stats"][:, bass.ds(n, 1), :].rearrange("p o s -> p (o s)"), Hst(Hs, n))

            def weigh(b, j, i, e, x, to, ready, count):
                dve.wait_ge(g[ready], START + b * TPB + j + 1)
                ch.link(nc.vector.reciprocal(SM[:, i, j:j + 1], SM[:, i, j:j + 1]))
                nc.vector.scalar_tensor_tensor(out=to, in0=e, scalar=SM[:, i, j:j + 1], in1=x, op0=ALU.mult, op1=ALU.mult).then_inc(g[count], 1)

            def body(b, u, fixed):
                ch.begin(PRE + 4 * TPB + b * 5 * TPB - (2 * TPB if fixed == B - 1 else 0))
                for j in range(TPB):
                    dve.wait_ge(g["kv_done"], START + b * TPB + j + 1)
                    nc.vector.tensor_reduce(out=NM[:, 0, j:j + 1], in_=QA[:, u, j, 1, :], op=ALU.max, axis=AX.X, negate=True).then_inc(g["max1_done"], 1)
                for j in range(TPB):
                    weigh(b, j, 0, QA[:, u, j, 1, :], QA[:, u, j, 0, :], WQ[:, j, :], "exp1_done", "wq_done")
                more = fixed is None or fixed < B - 1
                for j in range(TPB):
                    dve.wait_ge(g["cum1_done"], START + b * TPB + j + 1)
                    nc.vector.scalar_tensor_tensor(out=Mx[:, j, :], in0=ps[:, turn_bank(u, j), 0:D], scalar=K[:, C_INV + j:C_INV + j + 1], in1=KV[:, u, j, 0, :], op0=ALU.mult, op1=ALU.mult).then_inc(g["m_done"], 1)
                if more:
                    add_biases(b + 1, 1 - u, 0)
                if fixed is None or fixed < B - 2:
                    norm_rows(b + 2, u)
                if more:
                    add_biases(b + 1, 1 - u, 1)
                for j in range(TPB):
                    n = b * TPB + j
                    dve.wait_ge(g["klog_done"], START + n + 1)
                    nc.vector.tensor_tensor(out=KL[:, j, :], in0=ps[:, turn_bank(u, TPB + j), 0:D], in1=BKA[:], op=ALU.add).then_inc(g["kl_done"], 1)
                    dve.wait_ge(g["kl_done"], START + n + 1)
                    nc.vector.tensor_reduce(out=NM[:, 1, j:j + 1], in_=KL[:, j, :], op=ALU.max, axis=AX.X, negate=True).then_inc(g["max2_done"], 1)
                for j in range(TPB):
                    weigh(b, j, 1, KL[:, j, :], Mx[:, j, :], KW[:, j, :], "exp2_done", "kw_done")
                if more:
                    add_biases(b + 1, 1 - u, 2)
                for j in range(TPB):
                    n = b * TPB + j
                    dve.wait_ge(g["cum2_done"], START + n + 1)
                    ch.link(nc.vector.scalar_tensor_tensor(out=TM[:, j, :], in0=ps[:, turn_bank(u, 2 * TPB + j), 0:D], scalar=K[:, C_INV + j:C_INV + j + 1], in1=KV[:, u, j, 1, :], op0=ALU.mult, op1=ALU.mult))
                    nc.vector.tensor_tensor(out=Hst(Hs, n), in0=TM[:, j, :], in1=Hst(Hs, n), op=ALU.add).then_inc(g["attn_out"], 1)
                    if j > 0:
                        out_stats(b, j - 1)
                out_stats(b, TPB - 1)
                ch.end(5 * TPB if fixed is None or fixed < B - 2 else 3 * TPB)

            def before():
                norm_rows(0, 0)
                norm_rows(1, 1)
                for j in range(TPB):
                    add_biases(0, 0, j)

            ch.begin(PRE)
            steps(dve, before, body)


def router_phase(s, made):
    sem = s["sem"]
    if made is None:
        names = ["zeros_set", "xd_zeroed", "wg_load", "rvar_done", "rrstd_done", "r_rows", "r_tr", "rt_done", "r_kept", "logit_mm", "gap_done", "gap_exp", "picks_done",
                 "rank_mm", "slots_done", "sw_scattered", "router_chain", "first_hi"]
        return {n: sem(n) for n in names}
    g = made
    nc, a, K, ident, Hs, ps, sb = s["nc"], s["a"], s["K"], s["ident"], s["Hs"], s["ps"], s["sb"]
    SI, GI, WT = s["scatter_at"], s["gather_at"], s["mix_weights"]
    R = 4
    NS = TOPK * NT
    Z0 = sb("zeros", [P, 15, D])
    WG = sb("w_gate", [P, DC, E])
    xp = s["expert_phase"]
    WS = s["expert_w"]["WS"]
    first_w = [[v[:].rearrange("p c n -> p (c n)") for v in s["expert_w"][x]] for x in ("FC", "PJ")]
    X3 = sb("x_norm", [P, NT, D])
    U = sb("r_rows_ring", [P, R, D])
    UT = sb("r_rowsT", [P, R, DC, P])
    ST = s["out_stats"]
    MV = sb("r_mv", [P, NT, 2])
    VE = sb("r_ve", [P, NT])
    RS = sb("r_rs", [P, NT])
    LG = sb("logits", [P, NT, E])
    REV = sb("reversed_index", [P, E])
    TP = sb("top", [P, TOPK, NT])
    EQ = sb("r_eq", [P, NT, E])
    IX = sb("r_ix", [P, NT])
    OH = sb("onehot", [P, TOPK, NT, E])
    GAP = sb("gap", [P, NT])
    TOT = sb("totals", [P, NS, E])
    INC = sb("running", [P, NS, E])
    ZZ = sb("zero_row", [P, NS])
    KO = sb("kept_onehot", [P, NS, E])
    KEPT = sb("kept", [P, NS])
    SL = sb("slots", [P, NS])
    SC = sb("slots_scatter", [P, NS])

    blk = nc.Block()
    with blk:
        @blk.sync
        def _(sp):
            sp.dma_start(WG[:], a["L0_ffn_w_g"].rearrange("(c p) e -> p c e", p=P)).then_inc(g["wg_load"], 16)
            load_expert(sp, s, 0)
            sp.wait_ge(g["zeros_set"], START + 1)
            for i in range(4):
                sp.dma_start(s["xd"][i * 15 * P:(i + 1) * 15 * P, :].rearrange("(p r) d -> p r d", p=P), Z0[:]).then_inc(g["xd_zeroed"], 16)

        @blk.gpsimd
        def _(pool):
            pool.wait_ge(g["rvar_done"], START + 1)
            nc.gpsimd.tensor_tensor(out=RS[:], in0=VE[:], in1=K[:, C_NHALF:C_NHALF + 1].to_broadcast([P, NT]), op=ALU.pow).then_inc(g["rrstd_done"], 1)
            pool.memset(Z0[:], 0.0).then_inc(g["zeros_set"], 1)
            pool.wait_ge(g["xd_zeroed"], START + 64)
            pool.wait_ge(g["r_kept"], START + NT)
            pool.wait_ge(g["slots_done"], START + 1)
            for k in range(TOPK):
                for i in range(NT):
                    pool.indirect_dma_start(out=s["xd"], out_offset=bass.IndirectOffsetOnAxis(ap=SI[:, k * NT + i:k * NT + i + 1], axis=0),
                                            in_=X3[:, i, :], in_offset=None).then_inc(g["sw_scattered"], 16)
            pool.wait_ge(g["sw_scattered"], 16 * NS)

        @blk.tensor
        def _(pe):
            pe.wait_ge(g["wg_load"], START + 16)
            with pe.Fori(0, NT // R) as q:
                for r in range(R):
                    n = q * R + r
                    pe.wait_ge(g["r_rows"], START + n + 1)
                    pe.wait_ge(g["rt_done"], START + n - 1)
                    for c in range(DC):
                        last = nc.tensor.transpose(ps[:, r % 2, c * P:(c + 1) * P], U[:, r, c * P:(c + 1) * P], ident)
                    last.then_inc(g["r_tr"], 1)
                for r in range(R):
                    n = q * R + r
                    pe.wait_ge(g["rt_done"], START + n + 1)
                    for c in range(DC):
                        last = nc.tensor.matmul(ps[:, 2, bass.ds(n * E, E)], UT[:, r, c, :], WG[:, c, :], start=(c == 0), stop=(c == DC - 1))
                    last.then_inc(g["logit_mm"], 1)
            pe.wait_ge(g["picks_done"], START + 1)
            oh = OH[:].rearrange("p k t e -> p (k t e)")
            nc.tensor.matmul(ps[:, 3, 0:NS * E], s["stri"], oh, start=True, stop=True)
            nc.tensor.matmul(ps[:, 4, 0:NS * E], s["ones"], oh, start=True, stop=True).then_inc(g["rank_mm"], 1)

        @blk.scalar
        def _(act):
            with act.Fori(0, NT // R) as q:
                for r in range(R):
                    n = q * R + r
                    act.wait_ge(g["r_tr"], START + n + 1)
                    act.wait_ge(g["logit_mm"], START + n - 3)
                    nc.scalar.activation(UT[:, r, :, :].rearrange("p c n -> p (c n)"), ps[:, r % 2, 0:D], ACT.Copy).then_inc(g["rt_done"], 1)
                    nc.scalar.activation(Hst(X3, n), U[:, r, :], ACT.Copy).then_inc(g["r_kept"], 1)
            act.wait_ge(g["gap_done"], START + 1)
            nc.scalar.activation(GAP[:], GAP[:], ACT.Exp).then_inc(g["gap_exp"], 1)
            for x in range(2):
                act.wait_ge(xp[f"ew_loaded{x}"], START + 16)
                nc.scalar.activation(first_w[x][0], WS[:, x, :], ACT.Copy).then_inc(g["first_hi"], 1)

        @blk.vector
        def _(dve):
            ch = Chain(dve, g["router_chain"])
            ch.begin(0)
            for n in range(NT):
                last = nc.vector.bn_aggr(MV[:, n, :], ST[:, n, :])
            ch.link(last)
            nc.vector.tensor_scalar(out=VE[:], in0=MV[:, :, 1], scalar1=EPS, scalar2=None, op0=ALU.add).then_inc(g["rvar_done"], 1)
            dve.wait_ge(g["rrstd_done"], START + 1)
            with dve.Fori(0, NT // R) as q:
                for r in range(R):
                    n = q * R + r
                    dve.wait_ge(g["r_kept"], START + n - 3)
                    dve.wait_ge(g["r_tr"], START + n - 3)
                    nc.vector.tensor_scalar(out=U[:, r, :], in0=Hst(Hs, n), scalar1=MV[:, bass.ds(n, 1), 0:1].rearrange("p o s -> p (o s)"),
                                            scalar2=RS[:, bass.ds(n, 1)], op0=ALU.subtract, op1=ALU.mult).then_inc(g["r_rows"], 1)
            dve.wait_ge(g["logit_mm"], START + NT)
            ch.link(nc.vector.tensor_copy(LG[:].rearrange("p t e -> p (t e)"), ps[:, 2, 0:NT * E]))
            ch.link(nc.vector.tensor_scalar(out=REV[:], in0=K[:, C_IOTA:C_IOTA + E], scalar1=-1.0, scalar2=float(E), op0=ALU.mult, op1=ALU.add))
            ch.link(nc.vector.memset(ZZ[:], 0.0))
            rev = REV[:, None, :].to_broadcast([P, NT, E])
            for k in range(TOPK):
                ch.link(nc.vector.tensor_reduce(out=TP[:, k, :], in_=LG[:], op=ALU.max, axis=AX.X))
                ch.link(nc.vector.tensor_tensor(out=EQ[:], in0=LG[:], in1=TP[:, k, :, None].to_broadcast([P, NT, E]), op=ALU.is_equal))
                ch.link(nc.vector.tensor_tensor(out=EQ[:], in0=EQ[:], in1=rev, op=ALU.mult))
                ch.link(nc.vector.tensor_reduce(out=IX[:], in_=EQ[:], op=ALU.max, axis=AX.X))
                ch.link(nc.vector.tensor_tensor(out=OH[:, k, :, :], in0=rev, in1=IX[:, :, None].to_broadcast([P, NT, E]), op=ALU.is_equal))
                if k == 0:
                    ch.link(nc.vector.tensor_scalar(out=EQ[:], in0=OH[:, 0, :, :], scalar1=-1.0, scalar2=1.0, op0=ALU.mult, op1=ALU.add))
                    ch.link(nc.vector.tensor_tensor(out=LG[:], in0=LG[:], in1=EQ[:], op=ALU.mult))
                    ch.link(nc.vector.tensor_scalar(out=EQ[:], in0=OH[:, 0, :, :], scalar1=-3e38, scalar2=None, op0=ALU.mult))
                    ch.link(nc.vector.tensor_tensor(out=LG[:], in0=LG[:], in1=EQ[:], op=ALU.add))
            nc.vector.sem_inc(g["picks_done"], 1)
            nc.vector.tensor_tensor(out=GAP[:], in0=TP[:, 1, :], in1=TP[:, 0, :], op=ALU.subtract).then_inc(g["gap_done"], 1)
            dve.wait_ge(g["rank_mm"], START + 1)
            ch.link(nc.vector.tensor_copy(TOT[:].rearrange("p s e -> p (s e)"), ps[:, 4, 0:NS * E]))
            for e in range(E):
                last = nc.vector.tensor_tensor_scan(out=INC[:, :, e], data0=TOT[:, :, e], data1=ZZ[:], initial=0.0, op0=ALU.add, op1=ALU.add)
            ch.link(last)
            ch.link(nc.vector.tensor_tensor(out=INC[:], in0=INC[:], in1=TOT[:], op=ALU.subtract))
            ch.link(nc.vector.tensor_tensor(out=INC[:].rearrange("p s e -> p (s e)"), in0=ps[:, 3, 0:NS * E], in1=INC[:].rearrange("p s e -> p (s e)"), op=ALU.add))
            oh = OH[:].rearrange("p k t e -> p (k t) e")
            ch.link(nc.vector.scalar_tensor_tensor(out=KO[:].rearrange("p s e -> p (s e)"), in0=INC[:].rearrange("p s e -> p (s e)"), scalar=float(CAP), in1=OH[:].rearrange("p k t e -> p (k t e)"), op0=ALU.is_lt, op1=ALU.mult))
            ch.link(nc.vector.tensor_reduce(out=KEPT[:], in_=KO[:], op=ALU.add, axis=AX.X))
            ch.link(nc.vector.tensor_tensor(out=INC[:], in0=INC[:], in1=K[:, None, C_E960:C_E960 + E].to_broadcast([P, NS, E]), op=ALU.add))
            ch.link(nc.vector.tensor_tensor(out=INC[:], in0=INC[:], in1=KO[:], op=ALU.mult))
            ch.link(nc.vector.tensor_reduce(out=SL[:], in_=INC[:], op=ALU.add, axis=AX.X))
            ch.link(nc.vector.tensor_scalar(out=SC[:], in0=KEPT[:], scalar1=-1.0, scalar2=1.0, op0=ALU.mult, op1=ALU.add))
            ch.link(nc.vector.tensor_tensor(out=SC[:], in0=SC[:], in1=K[:, C_TRASH:C_PE], op=ALU.mult))
            ch.link(nc.vector.tensor_tensor(out=SC[:], in0=SC[:], in1=SL[:], op=ALU.add))
            ch.link(nc.vector.tensor_copy(GI[:], SL[:]))
            nc.vector.tensor_copy(SI[:], SC[:]).then_inc(g["slots_done"], 1)
            dve.wait_ge(g["gap_exp"], START + 1)
            ch.link(nc.vector.tensor_scalar(out=IX[:], in0=GAP[:], scalar1=1.0, scalar2=None, op0=ALU.add))
            ch.link(nc.vector.reciprocal(WT[:, 0, :], IX[:]))
            ch.link(nc.vector.tensor_tensor(out=WT[:, 1, :], in0=WT[:, 0, :], in1=GAP[:], op=ALU.mult))
            ch.link(nc.vector.tensor_tensor(out=WT[:].rearrange("p k t -> p (k t)"), in0=WT[:].rearrange("p k t -> p (k t)"), in1=KEPT[:], op=ALU.mult))
            for x in range(2):
                dve.wait_ge(g["first_hi"], START + x + 1)
                nc.vector.tensor_tensor(out=first_w[x][1], in0=WS[:, x, :], in1=first_w[x][0].bitcast(F32), op=ALU.subtract).then_inc(xp[f"w_split{x}"], 1)
                nc.vector.sem_inc(xp["w_hi"], 2)


def expert_phase(s, made):
    sem = s["sem"]
    if made is None:
        names = ["ew_loaded0", "ew_loaded1", "xe_loaded0", "xe_loaded1", "xe_tr", "xt_hi", "xt_done", "fc_mm", "w_hi", "pool_waited", "w_split0", "w_split1", "gelu_done", "g_hi", "g_split", "down_mm", "ye_done", "y_stored0", "y_stored1",
                 *(f"sw_gather{i}" for i in range(8)), "mix1_done", "mixed", "out_stored"]
        return {n: sem(n) for n in names}
    g = made
    nc, a, K, ident, Hs, ps, sb = s["nc"], s["a"], s["K"], s["ident"], s["Hs"], s["ps"], s["sb"]
    GI, WT = s["gather_at"], s["mix_weights"]
    TH = CTN // 2
    WS = s["expert_w"]["WS"]
    FC = [s["expert_w"]["FC"], [sb(f"w_fc_{x}1", [P, DC, M], F32R) for x in ("hi", "lo")]]
    PJ = [s["expert_w"]["PJ"], [sb(f"w_proj_{x}1", [P, MC, D], F32R) for x in ("hi", "lo")]]
    XE = sb("x_expert", [CT, 2, TH, D])
    XT = [sb(f"x_expertT_{x}", [P, 2, DC, HALF], F32R) for x in ("hi", "lo")]
    G4 = sb("gelu_raw", [P, 4, HALF])
    GH = [sb(f"gelu_{x}", [P, 2, MC, HALF], F32R) for x in ("hi", "lo")]
    YO = sb("y_rows", [CT, 2, TH, D])
    R = 8
    GA = WS[:].rearrange("p x n -> p (x n)").rearrange("p (r k d) -> p r k d", k=TOPK, d=D)
    PAIRS = ((0, 0), (0, 1), (1, 0))
    xd = s["xd"][0:SLOTS, :].rearrange("(s t p) d -> s p t d", t=TH, p=CT)
    yd = s["yd"].rearrange("(s t p) d -> s p t d", t=TH, p=CT)
    FCB = (2, 3, 4, 7)
    STEPS = 2 * E

    def steps(eng, body):
        with eng.Fori(0, STEPS // 4 - 1) as q:
            for i in range(4):
                body(q * 4 + i, i, q, i + 0)
        for i in range(4):
            body(STEPS - 4 + i, i, STEPS // 4 - 1, STEPS - 4 + i)

    blk = nc.Block()
    with blk:
        @blk.sync
        def _(sp):
            def step(n, i, q):
                h, e = i % 2, q * 2 + i // 2
                if h == 0 and not (isinstance(n, int) and n == 0):
                    sp.wait_ge(g["w_hi"], START + 4 * e)
                    load_expert(sp, s, e)
                sp.wait_ge(g["xe_tr"], START + 2 * n - 2)
                sp.dma_start(XE[:, h, :, :], xd[bass.ds(n, 1)].rearrange("o p t d -> p (o t) d")).then_inc(g[f"xe_loaded{h}"], 16)
                if not (isinstance(n, int) and n < 2):
                    store(n - 2, h)

            def store(n, h):
                sp.wait_ge(g["ye_done"], START + n * TH + TH)
                sp.dma_start(yd[bass.ds(n, 1)].rearrange("o p t d -> p (o t) d"), YO[:, h, :, :]).then_inc(g[f"y_stored{h}"], 16)

            for i in range(4):
                step(i, i, 0)
            with sp.Fori(1, STEPS // 4) as q:
                for i in range(4):
                    step(q * 4 + i, i, q)
            store(STEPS - 2, 0)
            store(STEPS - 1, 1)
            for i in range(NT):
                sp.wait_ge(g["mixed"], START + i + 1)
                sp.dma_start(s["out"][i // TPB, (i % TPB) * P:(i % TPB + 1) * P, :], Hs[:, i, :]).then_inc(g["out_stored"], 16)
            sp.wait_ge(g["out_stored"], START + 16 * NT)

        @blk.gpsimd
        def _(pool):
            def split(e, i):
                for x, to in enumerate((FC[i], PJ[i])):
                    hi, lo = (v[:].rearrange("p c n -> p (c n)") for v in to)
                    pool.wait_ge(g[f"ew_loaded{x}"], START + 16 * e + 16)
                    pool.wait_ge(g["down_mm"], START + e * CTN - CTN)
                    pool.sem_inc(g["pool_waited"], 1)
                    nc.gpsimd.tensor_copy(hi, WS[:, x, :]).then_inc(g["w_hi"], 1)
                    pool.wait_ge(g["w_hi"], START + 4 * e + 2 * x + 1)
                    nc.gpsimd.tensor_tensor(out=lo, in0=WS[:, x, :], in1=hi.bitcast(F32), op=ALU.subtract).then_inc(g["w_hi"], 1)
                    pool.wait_ge(g["w_hi"], START + 4 * e + 2 * x + 2)
                    pool.sem_inc(g[f"w_split{x}"], 1)

            split(1, 1)
            with pool.Fori(1, E // 2) as ep:
                for i in range(2):
                    split(ep * 2 + i, i)
            pool.wait_ge(g["y_stored0"], START + 16 * E)
            pool.wait_ge(g["y_stored1"], START + 16 * E)
            for i in range(NT):
                if i >= R:
                    pool.wait_ge(g["mixed"], START + i - R + 1)
                for k in range(TOPK):
                    pool.indirect_dma_start(out=GA[:, i % R, k, :], out_offset=None, in_=s["yd"],
                                            in_offset=bass.IndirectOffsetOnAxis(ap=GI[:, k * NT + i:k * NT + i + 1], axis=0)).then_inc(g[f"sw_gather{i % R}"], 16)

        @blk.tensor
        def _(pe):
            def columns(n, h, lp):
                pe.wait_ge(g[f"xe_loaded{h}"], START + 16 * lp + 16)
                for c in range(DC):
                    pe.wait_ge(g["xt_done"], START + 2 * n)
                    for t in range(TH):
                        last = nc.tensor.transpose(ps[:, c, t * CT:(t + 1) * CT], XE[:, h, t, c * P:(c + 1) * P], ident[0:CT, 0:CT])
                    last.then_inc(g["xe_tr"], 1)

            def up(n, h, slot, wl):
                pe.wait_ge(g["w_split0"], START + 2 * wl + slot + 1)
                pe.wait_ge(g["xt_done"], START + 2 * n + 2)
                for m in range(MC):
                    pe.wait_ge(g["gelu_done"], START + n * MC + (m - 3))
                    for c in range(DC):
                        for x, y in PAIRS:
                            last = nc.tensor.matmul(ps[:, FCB[m % 4], 0:HALF], FC[slot][x][:, c, m * P:(m + 1) * P], XT[y][:, h, c, :],
                                                    start=((c, x, y) == (0, 0, 0)), stop=((c, x) == (DC - 1, 1)))
                    last.then_inc(g["fc_mm"], 1)

            def down(n, h, slot, wl):
                pe.wait_ge(g["w_split1"], START + 2 * wl + slot + 1)
                for t in range(TH):
                    pe.wait_ge(g["g_split"], START + n * MC + MC)
                    pe.wait_ge(g["ye_done"], START + n * TH + (t - 1))
                    for m in range(MC):
                        for x, y in PAIRS:
                            last = nc.tensor.matmul(ps[0:CT, 5 + t % 2, 0:D], GH[x][:, h, m, t * CT:(t + 1) * CT], PJ[slot][y][:, m, :],
                                                    start=((m, x, y) == (0, 0, 0)), stop=((m, x) == (MC - 1, 1)))
                    last.then_inc(g["down_mm"], 1)

            def body(n, i, q, known):
                if not (isinstance(n, int) and n + 1 >= STEPS):
                    up(n + 1, (i + 1) % 2, ((i + 1) // 2) % 2, q + (i + 1) // 4)
                if not (isinstance(n, int) and n + 2 >= STEPS):
                    columns(n + 2, i % 2, q * 2 + (i + 2) // 2)
                down(n, i % 2, i // 2, q)

            columns(0, 0, 0)
            up(0, 0, 0, 0)
            columns(1, 1, 0)
            steps(pe, body)

        @blk.scalar
        def _(act):
            def body(n, i, q, known):
                h = i % 2
                act.wait_ge(g["down_mm"], START + n * TH - TH)
                for m in range(MC):
                    act.wait_ge(g["fc_mm"], START + n * MC + m + 1)
                    act.wait_ge(g["g_split"], START + n * MC + m - 3)
                    nc.scalar.activation(G4[:, m % 4, :], ps[:, FCB[m % 4], 0:HALF], ACT.Gelu).then_inc(g["gelu_done"], 1)
                    act.wait_ge(g["gelu_done"], START + n * MC + m + 1)
                    nc.scalar.activation(GH[0][:, h, m, :], G4[:, m % 4, :], ACT.Copy).then_inc(g["g_hi"], 1)
            steps(act, body)

        @blk.vector
        def _(dve):
            def rows_out(n, h, st):
                dve.wait_ge(g[f"y_stored{h}"], START + 16 * st)
                for t in range(TH):
                    dve.wait_ge(g["down_mm"], START + n * TH + t + 1)
                    nc.vector.tensor_copy(YO[:, h, t, :], ps[0:CT, 5 + t % 2, 0:D]).then_inc(g["ye_done"], 1)

            def columns_out(n, h):
                dve.wait_ge(g["fc_mm"], START + n * MC - MC)
                for c in range(DC):
                    dve.wait_ge(g["xe_tr"], START + 2 * n + (c + 1))
                    nc.vector.tensor_copy(XT[0][:, h, c, :], ps[:, c, 0:HALF]).then_inc(g["xt_hi"], 1)
                for c in range(DC):
                    dve.wait_ge(g["xt_hi"], START + 2 * n + (c + 1))
                    nc.vector.tensor_tensor(out=XT[1][:, h, c, :], in0=ps[:, c, 0:HALF], in1=XT[0][:, h, c, :].bitcast(F32), op=ALU.subtract).then_inc(g["xt_done"], 1)

            def split_gelu(n, h):
                dve.wait_ge(g["down_mm"], START + n * TH - TH)
                for m in range(MC):
                    dve.wait_ge(g["g_hi"], START + n * MC + m + 1)
                    nc.vector.tensor_tensor(out=GH[1][:, h, m, :], in0=G4[:, m % 4, :], in1=GH[0][:, h, m, :].bitcast(F32), op=ALU.subtract).then_inc(g["g_split"], 1)

            def body(n, i, q, known):
                if not (isinstance(n, int) and n + 1 >= STEPS):
                    split_gelu(n + 1, (i + 1) % 2)
                if not (isinstance(n, int) and n + 2 >= STEPS):
                    columns_out(n + 2, i % 2)
                rows_out(n, i % 2, q * 2 + i // 2)

            columns_out(0, 0)
            split_gelu(0, 0)
            columns_out(1, 1)
            steps(dve, body)
            for i in range(NT):
                dve.wait_ge(g[f"sw_gather{i % R}"], 32 * (i // R + 1))
                nc.vector.scalar_tensor_tensor(out=Hs[:, i, :], in0=GA[:, i % R, 0, :], scalar=WT[:, 0, i:i + 1], in1=Hs[:, i, :], op0=ALU.mult, op1=ALU.add).then_inc(g["mix1_done"], 1)
                dve.wait_ge(g["mix1_done"], START + i + 1)
                nc.vector.scalar_tensor_tensor(out=Hs[:, i, :], in0=GA[:, i % R, 1, :], scalar=WT[:, 1, i:i + 1], in1=Hs[:, i, :], op0=ALU.mult, op1=ALU.add).then_inc(g["mixed"], 1)




def _constants():
    import numpy as np
    k = np.zeros((P, C_ALL), np.float32)
    i = np.arange(P)
    k[:, C_ID:C_ID + P] = np.eye(P)
    k[:, C_TRI:C_TRI + P] = i[:, None] <= i[None, :]
    k[:, C_STRI:C_STRI + P] = i[:, None] < i[None, :]
    k[:, C_ONE:C_ONE + P] = 1.0
    k[:, C_EO] = (i % 32) < 16
    k[:, C_EO + 1] = (i % 32) >= 16
    for t in range(TPB):
        k[:, C_INV + t] = np.float32(1.0) / (t * P + i + 1).astype(np.float32)
    k[:, C_IOTA:C_IOTA + E] = np.arange(E)
    k[:, C_E960:C_E960 + E] = np.arange(E) * CAP
    k[:, C_TRASH:C_PE] = SLOTS + P * np.arange(TOPK * NT)[None, :] + i[:, None]
    k[:, C_NHALF] = -0.5
    pos = np.arange(L_TXT, dtype=np.float32)[:, None]
    div = np.exp(np.arange(0, D, 2, dtype=np.float32) * np.float32(-np.log(np.float32(10000.0)) / np.float32(D)))
    ang = (pos * div).astype(np.float32)
    k[:, C_PE:C_PE + D:2] = np.sin(ang)
    k[:, C_PE + 1:C_PE + D:2] = np.cos(ang)
    return k


def kernel(**inputs):
    import numpy as _np
    import concourse.bacc as _bacc
    from concourse import mybir as _mybir
    from concourse.bass_utils import run_bass_kernel_spmd as _run
    nc = _bacc.Bacc("TRN2", target_bir_lowering=False, num_devices=1)
    arrays, a = {}, {}
    inputs = dict(inputs)
    inputs["const"] = _constants()
    for name, v in inputs.items():
        v = _np.ascontiguousarray(v)
        if v.dtype == _np.bool_:
            v = v.view(_np.int32)
        arrays[f"in_{name}"] = v
        a[name] = nc.dram_tensor(f"in_{name}", v.shape, _mybir.dt.from_np(v.dtype), kind="ExternalInput").ap()
    out = nc.dram_tensor("out", (B, TPB * P, D), F32, kind="ExternalOutput").ap()
    program(nc, a, out)
    r = _run(nc, [arrays], core_ids=[0])
    return r.results[0]["out"]
```
